# Optimizing a Trainium2 kernel written in Bass

```python
import numpy as np
import jax
import jax.numpy as jnp

def _softmax(x, axis=-1):
    return jax.nn.softmax(x, axis=axis)

def _gelu(x):
    return jax.nn.gelu(x, approximate=True)

def _silu(x):
    return jax.nn.silu(x)

def _sigmoid(x):
    return jax.nn.sigmoid(x)

def _layernorm(x, axis=-1, eps=1e-05):
    m = jnp.mean(x, axis=axis, keepdims=True)
    v = jnp.var(x, axis=axis, keepdims=True)
    return (x - m) / jnp.sqrt(v + eps)

def _scatter_add(tgt, idx, src, axis=0):
    return tgt.at[idx].add(src)

def _segment_sum(src, seg, n):
    return jax.ops.segment_sum(src, seg, n)
kernel_name = 'mk_macaron_d1_jaxref_r8_ffa20f'

def setup_inputs(seed: int=0):
    np.random.seed(seed)
    _w = jnp.asarray

    def _L0_attn_setup():
        import jax, jax.numpy as jnp
        import numpy as np
        B, S, E, H = (2, 256, 128, 16)
        D = E // H
        key = jax.random.key(seed)
        ks = jax.random.split(key, 8)
        hidden_states = jax.random.normal(ks[0], (B, S, E), dtype=jnp.float32)
        Wq = jax.random.normal(ks[1], (E, E), dtype=jnp.float32) * 0.02
        Wk = jax.random.normal(ks[2], (E, E), dtype=jnp.float32) * 0.02
        Wv = jax.random.normal(ks[3], (E, E), dtype=jnp.float32) * 0.02
        bq = jnp.zeros((E,), jnp.float32)
        bk = jnp.zeros((E,), jnp.float32)
        bv = jnp.zeros((E,), jnp.float32)
        eye = jnp.eye(E, dtype=jnp.float32)
        Wfq = eye + jax.random.normal(ks[4], (E, E), dtype=jnp.float32) * 0.02
        Wfk = eye + jax.random.normal(ks[5], (E, E), dtype=jnp.float32) * 0.02
        bfq = jnp.zeros((E,), jnp.float32)
        bfk = jnp.zeros((E,), jnp.float32)
        return dict(hidden_states=hidden_states, Wq=Wq, bq=bq, Wk=Wk, bk=bk, Wv=Wv, bv=bv, Wfq=Wfq, bfq=bfq, Wfk=Wfk, bfk=bfk)
    _L0_attn_in = _L0_attn_setup()

    def _L0_ffn_setup():
        import jax, jax.numpy as jnp
        import numpy as np
        E = 32
        K = 4
        H = 128
        F = 128
        LIMIT = 7.0
        ALPHA = 1.702
        EPS = 1e-05

        def _rmsnorm(x, scale):
            t = x * jax.lax.rsqrt(jnp.mean(x * x, axis=-1, keepdims=True) + EPS)
            return t * scale

        def _swiglu(h):
            glu = jnp.minimum(h[..., ::2], LIMIT)
            lin = jnp.clip(h[..., 1::2], -LIMIT, LIMIT)
            return glu * jax.nn.sigmoid(ALPHA * glu) * (lin + 1.0)
        key = jax.random.key(seed)
        ks = jax.random.split(key, 8)
        B, S = (1, 128)
        x = jax.random.normal(ks[0], (B, S, H), dtype=jnp.float32)
        norm_scale = jnp.ones((H,), dtype=jnp.float32)
        gate_w = jax.random.normal(ks[1], (E, H), dtype=jnp.float32) * 0.02
        gate_b = jnp.zeros((E,), dtype=jnp.float32)
        w1 = jax.random.normal(ks[2], (E, 2 * F, H), dtype=jnp.float32) * 0.02
        b1 = jnp.zeros((E, 2 * F), dtype=jnp.float32)
        w2 = jax.random.normal(ks[3], (E, H, F), dtype=jnp.float32) * 0.02
        b2 = jnp.zeros((E, H), dtype=jnp.float32)
        return {'x': x, 'norm_scale': norm_scale, 'gate_w': gate_w, 'gate_b': gate_b, 'w1': w1, 'b1': b1, 'w2': w2, 'b2': b2}
    _L0_ffn_in = _L0_ffn_setup()
    _d = {'L0_attn_hidden_states': _L0_attn_in['hidden_states'], 'L0_attn_Wq': _L0_attn_in['Wq'], 'L0_attn_bq': _L0_attn_in['bq'], 'L0_attn_Wk': _L0_attn_in['Wk'], 'L0_attn_bk': _L0_attn_in['bk'], 'L0_attn_Wv': _L0_attn_in['Wv'], 'L0_attn_bv': _L0_attn_in['bv'], 'L0_attn_Wfq': _L0_attn_in['Wfq'], 'L0_attn_bfq': _L0_attn_in['bfq'], 'L0_attn_Wfk': _L0_attn_in['Wfk'], 'L0_attn_bfk': _L0_attn_in['bfk'], 'L0_ffn_norm_scale': _L0_ffn_in['norm_scale'], 'L0_ffn_gate_w': _L0_ffn_in['gate_w'], 'L0_ffn_gate_b': _L0_ffn_in['gate_b'], 'L0_ffn_w1': _L0_ffn_in['w1'], 'L0_ffn_b1': _L0_ffn_in['b1'], 'L0_ffn_w2': _L0_ffn_in['w2'], 'L0_ffn_b2': _L0_ffn_in['b2']}
    _x0 = _d['L0_attn_hidden_states']
    _d['L0_attn_hidden_states'] = jax.random.normal(jax.random.fold_in(jax.random.key(seed), 1), (16, 256, 128), dtype=_x0.dtype)
    del _x0
    return _d

def reference(L0_attn_hidden_states, L0_attn_Wq, L0_attn_bq, L0_attn_Wk, L0_attn_bk, L0_attn_Wv, L0_attn_bv, L0_attn_Wfq, L0_attn_bfq, L0_attn_Wfk, L0_attn_bfk, L0_ffn_norm_scale, L0_ffn_gate_w, L0_ffn_gate_b, L0_ffn_w1, L0_ffn_b1, L0_ffn_w2, L0_ffn_b2):

    def _L0_attn_ref(hidden_states, Wq, bq, Wk, bk, Wv, bv, Wfq, bfq, Wfk, bfk):
        import jax, jax.numpy as jnp
        import numpy as np
        B, S, E, H = (2, 256, 128, 16)
        D = E // H
        b, s, e = hidden_states.shape
        d = e // H
        q = jax.nn.softmax((hidden_states @ Wq.T + bq) @ Wfq.T + bfq, axis=-1)
        k = jax.nn.softmax((hidden_states @ Wk.T + bk) @ Wfk.T + bfk, axis=-1)
        v = hidden_states @ Wv.T + bv
        split = lambda t: t.reshape(b, s, H, d).transpose(0, 2, 1, 3)
        q, k, v = (split(q), split(k), split(v))
        scores = jnp.einsum('bhsd,bhtd->bhst', q, k)
        probs = scores / jnp.sum(scores, axis=-1, keepdims=True)
        ctx = jnp.einsum('bhst,bhtd->bhsd', probs, v)
        return ctx.transpose(0, 2, 1, 3).reshape(b, s, e)

    def _L0_ffn_ref(x, norm_scale, gate_w, gate_b, w1, b1, w2, b2):
        import jax, jax.numpy as jnp
        import numpy as np
        E = 32
        K = 4
        H = 128
        F = 128
        LIMIT = 7.0
        ALPHA = 1.702
        EPS = 1e-05

        def _rmsnorm(x, scale):
            t = x * jax.lax.rsqrt(jnp.mean(x * x, axis=-1, keepdims=True) + EPS)
            return t * scale

        def _swiglu(h):
            glu = jnp.minimum(h[..., ::2], LIMIT)
            lin = jnp.clip(h[..., 1::2], -LIMIT, LIMIT)
            return glu * jax.nn.sigmoid(ALPHA * glu) * (lin + 1.0)
        B, S, _ = x.shape
        t = _rmsnorm(x, norm_scale)
        g = t @ gate_w.T + gate_b
        tf = t.reshape(-1, H)
        gf = g.reshape(-1, E)
        T = tf.shape[0]
        vals, idx = jax.lax.top_k(gf, K)
        w = jax.nn.softmax(vals, axis=-1)
        combine = jnp.zeros((T, E), dtype=tf.dtype).at[jnp.arange(T)[:, None], idx].add(w)
        h1 = jnp.einsum('th,efh->tef', tf, w1) + b1
        h = _swiglu(h1)
        hw = h * combine[:, :, None]
        out = jnp.einsum('tef,ehf->th', hw, w2) + combine @ b2
        return x + out.reshape(B, S, H)
    x = L0_attn_hidden_states
    x = x + 0.5 * _L0_ffn_ref(_layernorm(x, axis=-1), L0_ffn_norm_scale, L0_ffn_gate_w, L0_ffn_gate_b, L0_ffn_w1, L0_ffn_b1, L0_ffn_w2, L0_ffn_b2)
    x = x + _L0_attn_ref(_layernorm(x, axis=-1), L0_attn_Wq, L0_attn_bq, L0_attn_Wk, L0_attn_bk, L0_attn_Wv, L0_attn_bv, L0_attn_Wfq, L0_attn_bfq, L0_attn_Wfk, L0_attn_bfk)
    x = x + 0.5 * _L0_ffn_ref(_layernorm(x, axis=-1), L0_ffn_norm_scale, L0_ffn_gate_w, L0_ffn_gate_b, L0_ffn_w1, L0_ffn_b1, L0_ffn_w2, L0_ffn_b2)
    return x

_drawn_inputs = setup_inputs


def setup_inputs(seed=0):
    import zlib

    import numpy as np

    out = dict(_drawn_inputs(seed))
    spreads = {'L0_attn_bq': (0.0, 0.1),
     'L0_attn_bk': (0.0, 0.1),
     'L0_attn_bv': (0.0, 0.1),
     'L0_attn_bfq': (0.0, 0.1),
     'L0_attn_bfk': (0.0, 0.1),
     'L0_ffn_norm_scale': (1.0, 0.2),
     'L0_ffn_gate_b': (0.0, 0.1),
     'L0_ffn_b1': (0.0, 0.1),
     'L0_ffn_b2': (0.0, 0.1)}
    factors = {}
    for name, (base, spread) in spreads.items():
        noise = np.random.default_rng([zlib.crc32(name.encode()), seed]).standard_normal(out[name].shape)
        drawn = base * np.exp(spread * noise) if base else spread * noise
        out[name] = jnp.asarray(drawn.astype(out[name].dtype))
    for name, factor in factors.items():
        out[name] = (out[name] * factor).astype(out[name].dtype)
    return out
```

```python
from contextlib import ExitStack

import concourse.bass as bass
from concourse import mybir


P = 128
H = 128
NTOK = 4096
NTILE = NTOK // P
NCHUNK = 2
CT = NTILE // NCHUNK
NE = 32
TOPK = 4
PAIRS = CT * TOPK
GT = 4
ST = -(-(CT * TOPK + NE - 1) // (2 * GT)) * 2 * GT
NG = ST // GT
GW = GT * H
SLOTS = ST * P
NB = CT // 2
NHEAD = 16
HD = H // NHEAD
EPS = 1e-5
LIMIT = 7.0
NPHASE = 2 * NCHUNK
NRG = CT // GT
CG = 4
NCG = CT // CG
KVW = H + NHEAD
STORE_LAG = 5

ALU = mybir.AluOpType
ACT = mybir.ActivationFunctionType
F32 = mybir.dt.float32
BF16 = mybir.dt.bfloat16
I32 = mybir.dt.int32
U32 = mybir.dt.uint32
X_AXIS = mybir.AxisListType.X


def sweep(eng, lead, n, tail, body):
    for k in range(lead):
        body(k, k % 2, k // 2)
    with eng.Fori(0, (n - lead) // 2) as i:
        for r in range(2):
            body(i * 2 + (lead + r), r, i + lead // 2)
    for k in range(n, n + tail):
        body(k, k % 2, k // 2)


def live(k, lag, n):
    return not isinstance(k, int) or 0 <= k - lag < n


def wait_count(eng, sem, count):
    if not isinstance(count, int) or count > 0:
        eng.wait_ge(sem, count)


def build(nc, x, wq, bq, wk, bk, wvT, bv, wfqT, bfq, wfkT, bfk,
          nscale, gwT, gate_b, w1T, b1, w2T, b2, out, xs, ys):
    with ExitStack() as ctx:
        def sb(name, shape, dt=F32):
            return ctx.enter_context(nc.sbuf_tensor(name, shape, dt))

        def sem(name):
            return ctx.enter_context(nc.semaphore(name))

        X = sb("X", [P, NTILE * H])
        U = sb("U", [P, NTILE * H])
        W1 = sb("W1", [P, NE * 2 * H])
        W2 = sb("W2", [P, NE * H])
        YG = sb("YG", [P, PAIRS, H])
        xrow = sb("xrow", [P, 2, GW])
        xT = sb("xT", [P, 2, GW])
        glu = sb("glu", [P, 2, GW])
        lin = sb("lin", [P, 2, GW])
        swish = sb("swish", [P, 2, GW])
        hid = sb("hid", [P, 2, GW])
        hidT = sb("hidT", [P, 2, GW])
        yrow = sb("yrow", [P, 2, GW])
        ident = sb("ident", [P, P])
        before = sb("before", [P, P], BF16)
        ones = sb("ones", [P, P], BF16)
        ones_f = sb("ones_f", [1, P])
        parts_on = sb("parts_on", [96, P], BF16)
        expert_no = sb("expert_no", [P, NE])
        slot_no = sb("slot_no", [96, ST])
        steps128 = sb("steps128", [NE, CT])
        starts3 = sb("starts3", [NE, 96], BF16)
        ends3 = sb("ends3", [NE, 96], BF16)
        starts128 = sb("starts128", [NE, NE], BF16)
        headblock = sb("headblock", [P, H])
        headcol = sb("headcol", [P, NHEAD])
        scale_col = sb("scale_col", [P, 1])
        gw = sb("gw", [P, NE])
        gb = sb("gb", [1, NE])
        bias_f = sb("bias_f", [96, 3 * H])
        bias_r = sb("bias_r", [96, 3 * H])
        bias_p = sb("bias_p", [96, 3 * H], BF16)
        wq_s = sb("wq_s", [P, H])
        wk_s = sb("wk_s", [P, H])
        wfq_s = sb("wfq_s", [P, H])
        wfk_s = sb("wfk_s", [P, H])
        bqk_s = sb("bqk_s", [P, 2])
        qkvW = sb("qkvW", [P, 3 * H])
        abias_f = sb("abias_f", [96, 3 * H])
        abias_r = sb("abias_r", [96, 3 * H])
        abias_p = sb("abias_p", [96, 3 * H], BF16)
        st = sb("st", [P, CT * 6])
        sum2 = sb("sum2", [P, CT])
        dif = sb("dif", [P, CT])
        var = sb("var", [P, CT])
        vq = sb("vq", [P, 2 * CT])
        rs = sb("rs", [P, 2 * CT])
        nshift = sb("nshift", [P, CT])
        bscale = sb("bscale", [P, CT])
        bshift = sb("bshift", [P, CT])
        tT = xT
        logits = sb("logits", [P, CT * NE])
        top = sb("top", [P, CT * 8])
        topi = sb("topi", [P, CT * 8], U32)
        topf = sb("topf", [P, PAIRS])
        chosen = sb("chosen", [P, PAIRS * NE])
        mask = sb("mask", [P, CT * NE], BF16)
        counts = sb("counts", [NE, 1])
        over = sb("over", [NE, CT])
        ntiles = sb("ntiles", [NE, 1], BF16)
        span = sb("span", [96, 2])
        started = sb("started", [96, ST])
        ended = sb("ended", [NE, ST], BF16)
        sel = sb("sel", [96, NCHUNK * ST], BF16)
        eid = sb("eid", [1, NCHUNK * ST], I32)
        base = sb("base", [P, NE])
        where = sb("where", [P, CT * NE])
        pos = sb("pos", [P, PAIRS], I32)
        pos_a = sb("pos_a", [P, PAIRS], I32)
        pos_b = sb("pos_b", [P, PAIRS], I32)
        row = sb("row", [P, NCHUNK * PAIRS], I32)
        dlog = sb("dlog", [P, PAIRS])
        elog = sb("elog", [P, PAIRS])
        esum = sb("esum", [P, CT])
        erec = sb("erec", [P, CT])
        wtop = sb("wtop", [P, NCHUNK * PAIRS])
        arow = sb("arow", [P, 2, 2 * H])
        aT = sb("aT", [P, 2, 2 * H])
        nmax = sb("nmax", [P, 2, 4])
        esm = sb("esm", [P, 2, 4, H])
        ssum = sb("ssum", [P, 2, 4])
        srec = sb("srec", [P, 2, 4])
        qk = sb("qk", [P, 2, 4, H])
        vext = sb("vext", [P, 2, 2, H + 2])
        qT = sb("qT", [P, 2, 2 * H])
        kvd = sb("kvd", [P, 2, KVW])
        drec = sb("drec", [P, 2, NHEAD])
        ctxs = sb("ctxs", [P, 2, H])

        PS = ctx.enter_context(nc.psum_tensor("PS", [P, 8, 512], F32))
        TP = [PS[:, 0, :], PS[:, 1, :]]
        H1 = [PS[:, 2:4, :].rearrange("p a n -> p (a n)"), PS[:, 4:6, :].rearrange("p a n -> p (a n)")]
        HT = PS[:, 6, :]
        YP = PS[:, 7, :]
        LOG = PS[:, 2, :]
        RANK = PS[:, 3, :]
        CNT = PS[0:NE, 4, 0:1]
        SPAN = PS[0:96, 4, 2:4]
        BASE = PS[:, 4, 4:4 + NE]
        EID = PS[0:1, 4, 64:64 + ST]
        KV = PS[:, 6, 0:H + 2]
        CTX = PS[:, 7, 0:2 * KVW].rearrange("p (a n) -> p a n", a=2)

        x_loaded = [sem(f"x_loaded{c}") for c in range(NCHUNK)]
        small_loaded = sem("small_loaded")
        attn_loaded = sem("attn_loaded")
        w_loaded = sem("w_loaded")
        zero_ready = sem("zero_ready")
        filled = [sem(f"filled{c}") for c in range(NCHUNK)]
        const_step = sem("const_step")
        chain = sem("chain")
        stats_done = sem("stats_done")
        var_ready = sem("var_ready")
        std_ready = sem("std_ready")
        norm_ready = sem("norm_ready")
        u_done = sem("u_done")
        base_done = sem("base_done")
        uT_done = sem("uT_done")
        tT_done = sem("tT_done")
        logits_done = sem("logits_done")
        logits_copied = sem("logits_copied")
        top_done = sem("top_done")
        topi_done = sem("topi_done")
        dlog_ready = sem("dlog_ready")
        elog_ready = sem("elog_ready")
        mask_ready = sem("mask_ready")
        counted = sem("counted")
        ntiles_ready = sem("ntiles_ready")
        spans_done = sem("spans_done")
        ended_ready = sem("ended_ready")
        eid_done = sem("eid_done")
        route_done = sem("route_done")
        scattered = [sem(f"scattered{c}") for c in range(NCHUNK)]
        xrow_loaded = [sem(f"xrow_loaded{r}") for r in range(2)]
        x_turned = sem("x_turned")
        xT_ready = sem("xT_ready")
        h1_done = sem("h1_done")
        glu_ready = sem("glu_ready")
        lin_ready = sem("lin_ready")
        swish_ready = sem("swish_ready")
        hid_ready = sem("hid_ready")
        hid_turned = sem("hid_turned")
        hidT_ready = sem("hidT_ready")
        y_done = sem("y_done")
        yrow_ready = sem("yrow_ready")
        yrow_stored = [sem(f"yrow_stored{r}") for r in range(2)]
        gathered = [sem(f"gathered{g}") for g in range(NCG)]
        combined = sem("combined")
        fold_done = sem("fold_done")
        fold_copied = sem("fold_copied")
        bias_ready = sem("bias_ready")
        arow_ready = sem("arow_ready")
        a_turned = sem("a_turned")
        aT_ready = sem("aT_ready")
        qkv_done = sem("qkv_done")
        nmax_ready = sem("nmax_ready")
        esm_ready = sem("esm_ready")
        v_copied = sem("v_copied")
        qk_ready = sem("qk_ready")
        q_turned = sem("q_turned")
        qT_ready = sem("qT_ready")
        kv_done = sem("kv_done")
        kvd_ready = sem("kvd_ready")
        ctx_done = sem("ctx_done")
        drec_ready = sem("drec_ready")
        ctxs_ready = sem("ctxs_ready")
        srec_ready = sem("srec_ready")
        attn_done = sem("attn_done")
        based = sem("based")
        out_stored = sem("out_stored")

        x_v = x.rearrange("(c t p) h -> c p t h", c=NCHUNK, p=P)
        out_v = out.rearrange("(g t p) h -> g p t h", t=CG, p=P)
        xs_v = [a.rearrange("(g p q) h -> g p (q h)", p=P, q=GT) for a in xs]
        ys_v = [a.rearrange("(g p q) h -> g p (q h)", p=P, q=GT) for a in ys]
        zero = YG[:, 0:PAIRS // 2, :].rearrange("p a h -> p (a h)")
        ZW = PAIRS // 2 * H
        NZ = SLOTS * H // (P * ZW)
        assert NZ * P * ZW == SLOTS * H

        NSMALL, NATTN, NW = 3 + 6, 7 + 3, 2
        NCONST = 21

        block = ctx.enter_context(nc.Block())

        @block.sync
        def _(sp):
            sp.dma_start(X[:, 0:CT * H].rearrange("p (t h) -> p t h", h=H), x_v[0]).then_inc(x_loaded[0], 16)
            sp.dma_start(scale_col[:], nscale).then_inc(small_loaded, 16)
            sp.dma_start(gw[:], gwT).then_inc(small_loaded, 16)
            sp.dma_start(gb[:], gate_b).then_inc(small_loaded, 16)
            for r in range(3):
                sp.dma_start(bias_f[NE * r:NE * r + NE, 0:2 * H], b1).then_inc(small_loaded, 16)
                sp.dma_start(bias_f[NE * r:NE * r + NE, 2 * H:3 * H], b2).then_inc(small_loaded, 16)
            sp.wait_ge(zero_ready, 1)
            for c in range(NCHUNK):
                for z in range(NZ):
                    sp.dma_start(xs[c].rearrange("(z p a) h -> z p (a h)", z=NZ, p=P)[z], zero)\
                        .then_inc(filled[c], 16)
                if c == 0:
                    for d in range(1, NCHUNK):
                        sp.dma_start(X[:, d * CT * H:(d + 1) * CT * H].rearrange("p (t h) -> p t h", h=H),
                                     x_v[d]).then_inc(x_loaded[d], 16)
                    sp.dma_start(W1[:], w1T).then_inc(w_loaded, 16)
                    sp.dma_start(W2[:], w2T).then_inc(w_loaded, 16)

            def experts(ph):
                c, g0 = ph % NCHUNK, ph * NG

                def step(k, r, m):
                    if live(k, 0, NG):
                        wait_count(sp, x_turned, k + (g0 - 1))
                        sp.dma_start(xrow[:, r, :], xs_v[c][bass.ds(k, 1)].rearrange("g p n -> (g p) n"))\
                            .then_inc(xrow_loaded[r], 16)
                    if live(k, STORE_LAG, NG):
                        s = (r + STORE_LAG) % 2
                        sp.wait_ge(yrow_ready, k + (g0 - STORE_LAG + 1))
                        sp.dma_start(ys_v[c][bass.ds(k - STORE_LAG, 1)].rearrange("g p n -> (g p) n"), yrow[:, s, :])\
                            .then_inc(yrow_stored[s], 16)

                sp.wait_ge(scattered[c], 16 * PAIRS * (ph // NCHUNK + 1))
                sweep(sp, 6, NG, STORE_LAG, step)

            for ph in range(NPHASE):
                experts(ph)
            for c in range(NCHUNK):
                for g in range(NCG):
                    sp.wait_ge(combined, PAIRS * (NCHUNK + c) + CG * TOPK * (g + 1))
                    t = c * CT + g * CG
                    sp.dma_start(out_v[c * NCG + g], X[:, t * H:(t + CG) * H].rearrange("p (t h) -> p t h", h=H))\
                        .then_inc(out_stored, 16)
            sp.wait_ge(out_stored, 16 * NCHUNK * NCG)

        @block.gpsimd
        def _(pool):
            made = [0]

            def step(ins):
                made[0] += 1
                ins.then_inc(const_step, 1)

            g = nc.gpsimd
            step(g.memset(ident[:], 0.0))
            step(g.memset(before[:], 1.0))
            step(g.memset(starts3[:], 1.0))
            step(g.memset(ends3[:], 1.0))
            step(g.memset(starts128[:], 128.0))
            step(g.memset(headblock[:], 1.0))
            step(g.memset(headcol[:], 1.0))
            step(g.memset(ones[:], 1.0))
            step(g.memset(ones_f[:], 1.0))
            step(g.iota(expert_no[:], [[1, NE]], base=0, channel_multiplier=0, allow_small_or_imprecise_dtypes=True))
            step(g.iota(slot_no[:], [[1, ST]], base=0, channel_multiplier=0, allow_small_or_imprecise_dtypes=True))
            step(g.iota(steps128[:], [[P, CT]], base=0, channel_multiplier=0, allow_small_or_imprecise_dtypes=True))
            pool.wait_ge(const_step, made[0])
            step(g.affine_select(out=ident[:], in_=ident[:], compare_op=ALU.not_equal, fill=1.0, base=0,
                                 pattern=[[-1, P]], channel_multiplier=1))
            step(g.affine_select(out=before[:], in_=before[:], compare_op=ALU.is_ge, fill=0.0, base=-1,
                                 pattern=[[1, P]], channel_multiplier=-1))
            step(g.affine_select(out=starts3[:].rearrange("p (r f) -> p r f", r=3),
                                 in_=starts3[:].rearrange("p (r f) -> p r f", r=3), compare_op=ALU.is_ge, fill=0.0,
                                 base=-1, pattern=[[0, 3], [1, NE]], channel_multiplier=-1))
            step(g.affine_select(out=ends3[:].rearrange("p (r f) -> p r f", r=3),
                                 in_=ends3[:].rearrange("p (r f) -> p r f", r=3), compare_op=ALU.is_ge, fill=0.0,
                                 base=0, pattern=[[0, 3], [1, NE]], channel_multiplier=-1))
            step(g.affine_select(out=starts128[:], in_=starts128[:], compare_op=ALU.is_ge, fill=0.0,
                                 base=-1, pattern=[[1, NE]], channel_multiplier=-1))
            hb = headblock[:].rearrange("p (b d) -> p b d", d=HD)
            step(g.affine_select(out=hb, in_=hb, compare_op=ALU.is_ge, fill=0.0,
                                 base=0, pattern=[[-HD, NHEAD], [0, HD]], channel_multiplier=1))
            step(g.affine_select(out=headcol[:], in_=headcol[:], compare_op=ALU.is_ge, fill=0.0,
                                 base=0, pattern=[[-HD, NHEAD]], channel_multiplier=1))
            pool.wait_ge(const_step, made[0])
            step(g.affine_select(out=hb, in_=hb, compare_op=ALU.is_ge, fill=0.0,
                                 base=HD - 1, pattern=[[HD, NHEAD], [0, HD]], channel_multiplier=-1))
            step(g.affine_select(out=headcol[:], in_=headcol[:], compare_op=ALU.is_ge, fill=0.0,
                                 base=HD - 1, pattern=[[HD, NHEAD]], channel_multiplier=-1))
            assert made[0] == NCONST

            def scatter(ph):
                c = ph % NCHUNK
                pool.wait_ge(u_done, CT * (ph + 1))
                pool.wait_ge(route_done, ph + 1)
                if ph < NCHUNK:
                    pool.wait_ge(filled[c], 16 * NZ)
                for t in range(CT):
                    for k in range(TOPK):
                        i = c * PAIRS + t * TOPK + k
                        pool.indirect_dma_start(
                            out=xs[c], out_offset=bass.IndirectOffsetOnAxis(ap=row[:, i:i + 1], axis=0),
                            in_=U[:, (c * CT + t) * H:(c * CT + t + 1) * H], in_offset=None,
                        ).then_inc(scattered[c], 16)

            def gather(ph):
                c = ph % NCHUNK
                for r in range(2):
                    pool.wait_ge(yrow_stored[r], 16 * (NG // 2) * (ph + 1))
                if ph == 0:
                    for d in range(NCHUNK):
                        pool.wait_ge(filled[d], 16 * NZ)
                for t in range(CT):
                    if ph and t % CG == 0:
                        pool.wait_ge(combined, PAIRS * (ph - 1) + TOPK * (t + CG))
                    for k in range(TOPK):
                        i = c * PAIRS + t * TOPK + k
                        pool.indirect_dma_start(
                            out=YG[:, t * TOPK + k, :], out_offset=None,
                            in_=ys[c], in_offset=bass.IndirectOffsetOnAxis(ap=row[:, i:i + 1], axis=0),
                        ).then_inc(gathered[t // CG], 16)

            for f in range(2):
                for c in range(NCHUNK):
                    scatter(f * NCHUNK + c)
                for c in range(NCHUNK):
                    gather(f * NCHUNK + c)

        @block.scalar
        def _(act):
            a = nc.scalar
            for dst, src in ((wq_s, wq), (wk_s, wk), (wfq_s, wfqT), (wfk_s, wfkT)):
                act.dma_start(dst[:], src).then_inc(attn_loaded, 16)
            act.dma_start(qkvW[:, 2 * H:3 * H], wvT).then_inc(attn_loaded, 16)
            act.dma_start(bqk_s[:, 0:1], bq).then_inc(attn_loaded, 16)
            act.dma_start(bqk_s[:, 1:2], bk).then_inc(attn_loaded, 16)
            for n, src in enumerate((bfq, bfk, bv)):
                act.dma_start(abias_f[:, n * H:(n + 1) * H], src.partition_broadcast(96)).then_inc(attn_loaded, 16)

            def rows_to(m, dst, d0, t0, done):
                with act.Fori(0, CT // 4) as i:
                    for j in range(4):
                        t = i * 4 + j
                        a.activation(dst[:, bass.ds((t + d0) * H, H)], X[:, bass.ds((t + t0) * H, H)], ACT.Identity,
                                     scale=rs[:, bass.ds(t + m, 1)], bias=nshift[:, bass.ds(t, 1)]).then_inc(done, 1)

            def normalise(n):
                act.wait_ge(var_ready, n + 1)
                a.activation(vq[:], vq[:], ACT.Sqrt).then_inc(std_ready, 1)

            def route(ph, n):
                c = ph % NCHUNK
                normalise(n)
                act.wait_ge(norm_ready, n + 1)
                if ph >= NCHUNK:
                    act.wait_ge(scattered[c], 16 * PAIRS * (ph // NCHUNK))
                rows_to(CT, U, c * CT, c * CT, u_done)
                if ph == 0:
                    act.wait_ge(small_loaded, 16 * NSMALL)
                for q in range(NRG):
                    Q = ph * NRG + q
                    act.wait_ge(uT_done, Q + 1)
                    wait_count(act, logits_done, Q - 1)
                    a.activation(tT[:, q % 2, :], TP[q % 2], ACT.Copy, scale=scale_col[:, 0:1]).then_inc(tT_done, 1)
                act.wait_ge(logits_done, (ph + 1) * NRG)
                wait_count(act, route_done, ph)
                a.activation(logits[:], LOG, ACT.Copy).then_inc(logits_copied, 1)
                act.wait_ge(dlog_ready, ph + 1)
                a.activation(elog[:], dlog[:], ACT.Exp).then_inc(elog_ready, 1)

            def experts(ph):
                g0 = ph * NG

                def step(k, r, m):
                    s = 1 - r
                    if live(k, 0, NG):
                        act.wait_ge(x_turned, k + (g0 + 1))
                        wait_count(act, h1_done, k + (g0 - 1))
                        a.activation(xT[:, r, :], TP[r], ACT.Copy, scale=scale_col[:, 0:1]).then_inc(xT_ready, 1)
                    if live(k, 3, NG):
                        act.wait_ge(hid_turned, k + (g0 - 2))
                        wait_count(act, y_done, k + (g0 - 4))
                        a.activation(hidT[:, s, :], HT, ACT.Copy).then_inc(hidT_ready, 1)
                    if live(k, 1, NG):
                        act.wait_ge(glu_ready, k + g0)
                        wait_count(act, hid_ready, k + (g0 - 2))
                        a.activation(swish[:, s, :], glu[:, s, :], ACT.Gelu_apprx_sigmoid).then_inc(swish_ready, 1)

                sweep(act, 6, NG, 3, step)

            def attention(c, n):
                n0 = c * NB
                normalise(n)
                act.wait_ge(norm_ready, n + 1)

                def norm_rows(k, s):
                    wait_count(act, a_turned, k + (n0 - 1))
                    for i in range(2):
                        t = k * 2 + i
                        a.activation(arow[:, s, i * H:(i + 1) * H], X[:, bass.ds((t + c * CT) * H, H)], ACT.Identity,
                                     scale=rs[:, bass.ds(t, 1)], bias=nshift[:, bass.ds(t, 1)]).then_inc(arow_ready, 1)

                def step(k, r, m):
                    s = 1 - r
                    if live(k, 0, NB):
                        act.wait_ge(a_turned, k + (n0 + 1))
                        wait_count(act, qkv_done, k + (n0 - 1))
                        a.activation(aT[:, r, :], PS[:, 0, 0:2 * H], ACT.Copy).then_inc(aT_ready, 1)
                    if live(k, -1, NB):
                        norm_rows(k + 1, s)
                    if live(k, 1, NB):
                        act.wait_ge(nmax_ready, k + n0)
                        wait_count(act, qk_ready, k + (n0 - 2))
                        for i in range(4):
                            a.activation(esm[:, s, i, :], PS[:, 2 + 2 * s + i // 2, (i % 2) * H:(i % 2 + 1) * H], ACT.Exp,
                                         bias=nmax[:, s, i:i + 1], accum_out=ssum[:, s, i:i + 1]).then_inc(esm_ready, 1)
                        wait_count(act, kv_done, k + (n0 - 2))
                        a.activation(vext[:, s, :, 0:H], PS[:, 2 + 2 * s:4 + 2 * s, 2 * H:3 * H], ACT.Copy)\
                            .then_inc(v_copied, 1)
                    if live(k, 2, NB):
                        act.wait_ge(q_turned, k + (n0 - 1))
                        wait_count(act, ctx_done, k + (n0 - 3))
                        a.activation(qT[:, r, :], PS[:, 1, 0:2 * H], ACT.Copy).then_inc(qT_ready, 1)

                norm_rows(0, 0)
                sweep(act, 4, NB - 2, 5, step)

            norms = 0
            for c in range(NCHUNK):
                route(c, norms)
                norms += 1
            for c in range(NCHUNK):
                experts(c)
            for c in range(NCHUNK):
                attention(c, norms)
                route(NCHUNK + c, norms + 1)
                norms += 2
            for c in range(NCHUNK):
                experts(NCHUNK + c)

        @block.vector
        def _(dve):
            v = nc.vector
            linked = [0]

            def link(ins):
                linked[0] += 1
                ins.then_inc(chain, 1)
                dve.wait_ge(chain, linked[0])

            def normalise(n, t0, rows):
                with dve.Fori(0, CT // 4) as i:
                    for j in range(4):
                        t = i * 4 + j
                        v.bn_stats(st[:, bass.ds(t * 6, 6)], X[:, bass.ds((t + t0) * H, H)]).then_inc(stats_done, 1)
                dve.wait_ge(stats_done, CT * (n + 1))
                s6 = st[:].rearrange("p (t s) -> p s t", s=6)
                link(v.tensor_tensor(sum2[:], s6[:, 1, :], s6[:, 4, :], ALU.add))
                link(v.tensor_tensor(dif[:], s6[:, 1, :], s6[:, 4, :], ALU.subtract))
                link(v.tensor_tensor(var[:], s6[:, 2, :], s6[:, 5, :], ALU.add))
                link(v.scalar_tensor_tensor(dif[:], dif[:], 0.25, dif[:], ALU.mult, ALU.mult))
                link(v.scalar_tensor_tensor(var[:], var[:], 1.0 / H, dif[:], ALU.mult, ALU.add))
                link(v.tensor_scalar(vq[:, 0:CT], var[:], EPS, None, ALU.add))
                v.scalar_tensor_tensor(vq[:, CT:2 * CT], vq[:, 0:CT], EPS, var[:], ALU.mult, ALU.add)\
                    .then_inc(var_ready, 1)
                dve.wait_ge(std_ready, n + 1)
                link(v.reciprocal(rs[:], vq[:]))
                v.scalar_tensor_tensor(nshift[:], sum2[:], -0.5, rs[:, rows], ALU.mult, ALU.mult)\
                    .then_inc(norm_ready, 1)

            def route(ph, n):
                c = ph % NCHUNK
                normalise(n, c * CT, slice(CT, 2 * CT))
                link(v.tensor_scalar(bscale[:], rs[:, 0:CT], 0.5, 1.0, ALU.mult, ALU.add))
                link(v.scalar_tensor_tensor(bshift[:], sum2[:], -0.25, rs[:, 0:CT], ALU.mult, ALU.mult))
                dve.wait_ge(u_done, CT * (ph + 1))
                with dve.Fori(0, CT // 4) as i:
                    for j in range(4):
                        t = i * 4 + j
                        xt = X[:, bass.ds((t + c * CT) * H, H)]
                        v.tensor_scalar(xt, xt, bscale[:, bass.ds(t, 1)], bshift[:, bass.ds(t, 1)],
                                        ALU.mult, ALU.add).then_inc(base_done, 1)
                dve.wait_ge(logits_copied, ph + 1)
                for t in range(CT):
                    v.max(top[:, t * 8:t * 8 + 8], logits[:, t * NE:(t + 1) * NE]).then_inc(top_done, 1)
                for t in range(CT):
                    dve.wait_ge(top_done, CT * ph + t + 1)
                    v.max_index(topi[:, t * 8:t * 8 + 8], top[:, t * 8:t * 8 + 8], logits[:, t * NE:(t + 1) * NE])\
                        .then_inc(topi_done, 1)
                t8 = top[:].rearrange("p (t k) -> p t k", k=8)
                tk = [P, CT, TOPK]
                dl = dlog[:].rearrange("p (t k) -> p t k", k=TOPK)
                v.tensor_tensor(dl, t8[:, :, 0:TOPK], t8[:, :, 0:1].broadcast_to(tk), ALU.subtract)\
                    .then_inc(dlog_ready, 1)
                dve.wait_ge(topi_done, CT * (ph + 1))
                link(v.tensor_copy(topf[:].rearrange("p (t k) -> p t k", k=TOPK),
                                   topi[:].rearrange("p (t k) -> p t k", k=8)[:, :, 0:TOPK]))
                ch = chosen[:].rearrange("p (t e) -> p t e", e=NE)
                link(v.tensor_tensor(ch, expert_no[:].rearrange("p (o e) -> p o e", o=1).broadcast_to([P, PAIRS, NE]),
                                     topf[:].rearrange("p (t o) -> p t o", o=1).broadcast_to([P, PAIRS, NE]),
                                     ALU.is_equal))
                with nc.allow_low_precision(reason="sums of at most one 1"):
                    v.tensor_reduce(mask[:].rearrange("p (t e) -> p t e", e=NE),
                                    chosen[:].rearrange("p (t k e) -> p t e k", k=TOPK, e=NE), X_AXIS, ALU.add)\
                        .then_inc(mask_ready, 1)
                dve.wait_ge(counted, ph + 1)
                link(v.tensor_copy(counts[:], CNT))
                link(v.tensor_scalar(over[:], steps128[:], counts[:, 0:1], None, ALU.is_lt))
                with nc.allow_low_precision(reason="integers up to 16"):
                    v.tensor_reduce(ntiles[:], over[:], X_AXIS, ALU.add).then_inc(ntiles_ready, 1)
                dve.wait_ge(spans_done, ph + 1)
                link(v.tensor_copy(span[:], SPAN))
                v.tensor_scalar(ended[:], slot_no[0:NE, :], span[0:NE, 1:2], None, ALU.is_ge).then_inc(ended_ready, 1)
                link(v.tensor_scalar(started[:], slot_no[:], span[:, 0:1], None, ALU.is_ge))
                link(v.scalar_tensor_tensor(sel[:, c * ST:(c + 1) * ST], slot_no[:], span[:, 1:2], started[:],
                                            ALU.is_lt, ALU.mult))
                v.tensor_copy(base[:], BASE).then_inc(based, 1)
                dve.wait_ge(based, ph + 1)
                te = [P, CT, NE]
                link(v.tensor_tensor(where[:].rearrange("p (t e) -> p t e", e=NE),
                                     RANK.rearrange("p (t e) -> p t e", e=NE),
                                     base[:].rearrange("p (o e) -> p o e", o=1).broadcast_to(te), ALU.add))
                for k in range(TOPK):
                    link(v.tensor_tensor(chosen[:].rearrange("p (t k e) -> p k t e", k=TOPK, e=NE)[:, k],
                                         chosen[:].rearrange("p (t k e) -> p k t e", k=TOPK, e=NE)[:, k],
                                         where[:].rearrange("p (t e) -> p t e", e=NE), ALU.mult))
                with nc.allow_low_precision(reason="one integer and zeros"):
                    link(v.tensor_reduce(pos[:], chosen[:].rearrange("p (t e) -> p t e", e=NE), X_AXIS, ALU.add))
                link(v.tensor_scalar(pos_a[:], pos[:], P - 1, 2, ALU.bitwise_and, ALU.logical_shift_left))
                link(v.tensor_scalar(pos_b[:], pos[:], 7, GT - 1, ALU.logical_shift_right, ALU.bitwise_and))
                link(v.tensor_tensor(pos_a[:], pos_a[:], pos_b[:], ALU.bitwise_or))
                link(v.tensor_scalar(pos_b[:], pos[:], 9, 9, ALU.logical_shift_right, ALU.logical_shift_left))
                link(v.tensor_tensor(row[:, c * PAIRS:(c + 1) * PAIRS], pos_a[:], pos_b[:], ALU.bitwise_or))
                dve.wait_ge(elog_ready, ph + 1)
                el = elog[:].rearrange("p (t k) -> p t k", k=TOPK)
                link(v.tensor_reduce(esum[:], el, X_AXIS, ALU.add))
                link(v.reciprocal(erec[:], esum[:]))
                link(v.scalar_tensor_tensor(wtop[:, c * PAIRS:(c + 1) * PAIRS].rearrange("p (t k) -> p t k", k=TOPK), el,
                                            0.5, erec[:].rearrange("p (t o) -> p t o", o=1).broadcast_to(tk),
                                            ALU.mult, ALU.mult))
                dve.wait_ge(eid_done, ph + 1)
                v.tensor_scalar(eid[:, c * ST:(c + 1) * ST], EID, float(NE - 1), None, ALU.min).then_inc(route_done, 1)

            def split(src, rest, dst):
                link(v.tensor_copy(dst[:], src[:]))
                link(v.tensor_tensor(rest[:], src[:], dst[:], ALU.subtract))
                for q in (1, 2):
                    link(v.tensor_copy(dst[NE * q:NE * q + NE, :], rest[NE * q:NE * q + NE, :]))
                link(v.tensor_tensor(rest[64:96, :], rest[64:96, :], dst[64:96, :], ALU.subtract))
                v.tensor_copy(dst[64:96, :], rest[64:96, :]).then_inc(bias_ready, 1)

            def experts(ph):
                g0 = ph * NG

                def step(k, r, m):
                    s = 1 - r
                    h1 = H1[s].rearrange("p (q g f) -> p g q f", q=GT, g=2)
                    if live(k, 4, NG):
                        dve.wait_ge(y_done, k + (g0 - 3))
                        wait_count(dve, yrow_stored[r], (m + (g0 // 2 - 2)) * 16)
                        v.tensor_copy(yrow[:, r, :], YP).then_inc(yrow_ready, 1)
                    if live(k, 1, NG):
                        dve.wait_ge(h1_done, k + g0)
                        wait_count(dve, swish_ready, k + (g0 - 2))
                        v.tensor_scalar(glu[:, s, :].rearrange("p (q f) -> p q f", q=GT), h1[:, 0],
                                        LIMIT, None, ALU.min).then_inc(glu_ready, 1)
                        wait_count(dve, hid_ready, k + (g0 - 2))
                        v.tensor_scalar(lin[:, s, :].rearrange("p (q f) -> p q f", q=GT), h1[:, 1],
                                        -LIMIT, LIMIT, ALU.max, ALU.min).then_inc(lin_ready, 1)
                    if live(k, 1, NG):
                        dve.wait_ge(swish_ready, k + g0)
                        dve.wait_ge(lin_ready, k + g0)
                        wait_count(dve, hid_turned, k + (g0 - 2))
                        v.scalar_tensor_tensor(hid[:, s, :], lin[:, s, :], 1.0, swish[:, s, :], ALU.add, ALU.mult)\
                            .then_inc(hid_ready, 1)

                sweep(dve, 6, NG, 4, step)

            def combine(ph):
                c = ph % NCHUNK
                dve.wait_ge(base_done, CT * (ph + 1))
                for g in range(NCG):
                    dve.wait_ge(gathered[g], 16 * CG * TOPK * (ph + 1))
                    for k in range(TOPK):
                        for t in range(g * CG, g * CG + CG):
                            if k:
                                dve.wait_ge(combined, PAIRS * ph + CG * TOPK * g + CG * (k - 1) + t % CG + 1)
                            xt = X[:, (c * CT + t) * H:(c * CT + t + 1) * H]
                            w = c * PAIRS + t * TOPK + k
                            v.scalar_tensor_tensor(xt, YG[:, t * TOPK + k, :], wtop[:, w:w + 1], xt,
                                                   ALU.mult, ALU.add).then_inc(combined, 1)

            def attention(c, n):
                n0 = c * NB
                dve.wait_ge(combined, PAIRS * (c + 1))
                normalise(n, c * CT, slice(0, CT))

                def step(k, r, m):
                    s = 1 - r
                    if live(k, 1, NB):
                        dve.wait_ge(qkv_done, k + n0)
                        v.tensor_reduce(nmax[:, s, :].rearrange("p (a b) -> p a b", a=2),
                                        PS[:, 2 + 2 * s:4 + 2 * s, 0:2 * H].rearrange("p a (b h) -> p a b h", b=2),
                                        X_AXIS, ALU.max, negate=True).then_inc(nmax_ready, 1)
                    if live(k, 2, NB):
                        dve.wait_ge(kv_done, k + (n0 - 1))
                        wait_count(dve, ctx_done, k + (n0 - 3))
                        v.tensor_tensor(kvd[:, r, 0:H], KV[:, 0:H], headblock[:], ALU.mult).then_inc(kvd_ready, 1)
                        v.tensor_tensor(kvd[:, r, H:KVW], headcol[:], KV[:, H:H + 1].broadcast_to([P, NHEAD]),
                                        ALU.mult).then_inc(kvd_ready, 1)
                    if live(k, 3, NB):
                        dve.wait_ge(ctx_done, k + (n0 - 2))
                        v.reciprocal(drec[:], CTX[:, :, H:KVW]).then_inc(drec_ready, 1)
                        dve.wait_ge(drec_ready, k + (n0 - 2))
                        v.tensor_tensor(ctxs[:].rearrange("p a (h d) -> p a h d", d=HD),
                                        CTX[:, :, 0:H].rearrange("p a (h d) -> p a h d", d=HD),
                                        drec[:].rearrange("p a (h o) -> p a h o", o=1).broadcast_to([P, 2, NHEAD, HD]),
                                        ALU.mult).then_inc(ctxs_ready, 1)
                        dve.wait_ge(ctxs_ready, k + (n0 - 2))
                        xt = X[:, bass.ds((k - 3) * (2 * H) + c * CT * H, 2 * H)]
                        v.tensor_tensor(xt, xt, ctxs[:].rearrange("p a n -> p (a n)"), ALU.add).then_inc(attn_done, 1)
                    if live(k, 1, NB):
                        dve.wait_ge(esm_ready, (k + n0) * 4)
                        v.reciprocal(srec[:, s, :], ssum[:, s, :]).then_inc(srec_ready, 1)
                        dve.wait_ge(srec_ready, k + n0)
                        wait_count(dve, kv_done, k + (n0 - 2))
                        v.tensor_tensor(qk[:, s], esm[:, s],
                                        srec[:, s, :].rearrange("p (a o) -> p a o", o=1).broadcast_to([P, 4, H]),
                                        ALU.mult).then_inc(qk_ready, 1)

                sweep(dve, 4, NB, 3, step)
                dve.wait_ge(attn_done, n0 + NB)

            v.memset(YG[:, 0:PAIRS // 2, :], 0.0).then_inc(zero_ready, 1)
            link(v.memset(parts_on[:], 0.0))
            for r in range(3):
                link(v.memset(parts_on[NE * r:NE * r + 1, :], 1.0))
            for s in range(2):
                link(v.memset(vext[:, s, :, H:H + 2], 1.0))
            dve.wait_ge(x_loaded[0], 16)
            dve.wait_ge(const_step, NCONST)
            norms = 0
            for c in range(NCHUNK):
                if c:
                    dve.wait_ge(x_loaded[c], 16)
                route(c, norms)
                norms += 1
                if c == 0:
                    dve.wait_ge(small_loaded, 16 * NSMALL)
                    split(bias_f, bias_r, bias_p)
            dve.wait_ge(fold_done, 1)
            dve.wait_ge(attn_loaded, 16 * NATTN)
            v.tensor_copy(qkvW[:, 0:2 * H], PS[:, 6, 0:2 * H]).then_inc(fold_copied, 1)
            link(v.tensor_tensor(abias_f[:, 0:2 * H], abias_f[:, 0:2 * H], PS[0:96, 7, 0:2 * H], ALU.add))
            split(abias_f, abias_r, abias_p)
            for c in range(NCHUNK):
                experts(c)
            for c in range(NCHUNK):
                combine(c)
                attention(c, norms)
                route(NCHUNK + c, norms + 1)
                norms += 2
            for c in range(NCHUNK):
                experts(NCHUNK + c)
            for c in range(NCHUNK):
                combine(NCHUNK + c)

        @block.tensor
        def _(pe):
            te = nc.tensor

            def turn(dst, src, n):
                for q in range(n):
                    last = te.transpose(dst[:, q * P:(q + 1) * P], src[:, q * H:(q + 1) * H], ident[:])
                return last

            def route(ph):
                c = ph % NCHUNK
                for q in range(0, NRG, 2):
                    for r in range(2):
                        pe.wait_ge(u_done, CT * ph + (q + r + 1) * GT)
                        wait_count(pe, tT_done, ph * NRG + q + r - 1)
                        t0 = (c * CT + (q + r) * GT) * H
                        turn(TP[r], U[:, t0:t0 + GW], GT).then_inc(uT_done, 1)
                    for r in range(2):
                        pe.wait_ge(tT_done, ph * NRG + q + r + 1)
                        if q + r == 0:
                            wait_count(pe, logits_copied, ph)
                        for i in range(GT):
                            t = (q + r) * GT + i
                            lg = LOG[:, t * NE:(t + 1) * NE]
                            te.matmul(lg, ones_f[0:1, :], gb[0:1, :], start=True, stop=False)
                            last = te.matmul(lg, tT[:, r, i * P:(i + 1) * P], gw[:], start=False, stop=True)
                        last.then_inc(logits_done, 1)
                pe.wait_ge(mask_ready, ph + 1)
                wait_count(pe, route_done, ph)
                te.matmul(RANK, before[:], mask[:], start=True, stop=False)
                for i in range(CT - 1):
                    n = CT - 1 - i
                    te.matmul(RANK[:, (i + 1) * NE:CT * NE].rearrange("p (t e) -> p t e", e=NE), ones[:],
                              mask[:, i * NE:(i + 1) * NE].rearrange("p (o e) -> p o e", o=1).broadcast_to([P, n, NE]),
                              start=False, stop=(i == CT - 2))
                for i in range(CT):
                    last = te.matmul(CNT, mask[:, i * NE:(i + 1) * NE], ones[:, 0:1], start=(i == 0), stop=(i == CT - 1))
                last.then_inc(counted, 1)
                pe.wait_ge(ntiles_ready, ph + 1)
                te.matmul(SPAN[:, 0:1], starts3[:], ntiles[:], start=True, stop=True)
                te.matmul(SPAN[:, 1:2], ends3[:], ntiles[:], start=True, stop=True)
                te.matmul(BASE, ntiles[:, 0:1].broadcast_to([NE, P]), starts128[:], start=True, stop=True)\
                    .then_inc(spans_done, 1)
                pe.wait_ge(ended_ready, ph + 1)
                pe.wait_ge(based, ph + 1)
                te.matmul(EID, ones[0:NE, 0:1], ended[:], start=True, stop=True).then_inc(eid_done, 1)

            def experts(ph):
                c, g0 = ph % NCHUNK, ph * NG

                def experts_of(g):
                    _, es = nc.values_load_multi_w_load_instructions(
                        eid[0:1, bass.ds(g * GT + c * ST, GT)], engines=[te.engine], min_val=0, max_val=NE - 1)
                    return es

                def slot(g, q):
                    return sel[:, bass.ds(g * GT + (c * ST + q), 1)].broadcast_to([96, P])

                def step(k, r, m):
                    s = 1 - r
                    if live(k, 0, NG):
                        pe.wait_ge(xrow_loaded[r], (m + (g0 // 2 + 1)) * 16)
                        wait_count(pe, xT_ready, k + (g0 - 1))
                        turn(TP[r], xrow[:, r, :], GT).then_inc(x_turned, 1)
                    if live(k, 3, NG):
                        pe.wait_ge(hid_ready, k + (g0 - 2))
                        wait_count(pe, hidT_ready, k + (g0 - 3))
                        turn(HT, hid[:, s, :], GT).then_inc(hid_turned, 1)
                    if live(k, 1, NG):
                        es = experts_of(k - 1)
                        pe.wait_ge(xT_ready, k + g0)
                        wait_count(pe, glu_ready, k + (g0 - 2))
                        wait_count(pe, lin_ready, k + (g0 - 2))
                        for q in range(GT):
                            h1 = H1[s][:, q * 2 * H:(q + 1) * 2 * H]
                            te.matmul(h1, slot(k - 1, q), bias_p[:, 0:2 * H], start=True, stop=False)
                            last = te.matmul(h1, xT[:, s, q * P:(q + 1) * P], W1[:, bass.ds(es[q] * (2 * H), 2 * H)],
                                             start=False, stop=True)
                        last.then_inc(h1_done, 1)
                    if live(k, 3, NG):
                        es = experts_of(k - 3)
                        pe.wait_ge(hidT_ready, k + (g0 - 2))
                        wait_count(pe, yrow_ready, k + (g0 - 3))
                        for q in range(GT):
                            y = YP[:, q * H:(q + 1) * H]
                            te.matmul(y, slot(k - 3, q), bias_p[:, 2 * H:3 * H], start=True, stop=False)
                            last = te.matmul(y, hidT[:, s, q * P:(q + 1) * P], W2[:, bass.ds(es[q] * H, H)],
                                             start=False, stop=True)
                        last.then_inc(y_done, 1)

                sweep(pe, 4, NG, 3, step)

            def attention(c):
                n0 = c * NB

                def step(k, r, m):
                    s = 1 - r
                    if live(k, 0, NB):
                        pe.wait_ge(arow_ready, (k + (n0 + 1)) * 2)
                        wait_count(pe, aT_ready, k + n0)
                        turn(PS[:, 0, :], arow[:, r, :], 2).then_inc(a_turned, 1)
                    if live(k, 1, NB):
                        pe.wait_ge(aT_ready, k + n0)
                        wait_count(pe, v_copied, k + (n0 - 2))
                        for i in range(2):
                            o = PS[:, 2 + 2 * s + i, 0:3 * H]
                            te.matmul(o, parts_on[:], abias_p[:], start=True, stop=False)
                            last = te.matmul(o, aT[:, s, i * P:(i + 1) * P], qkvW[:], start=False, stop=True)
                        last.then_inc(qkv_done, 1)
                    if live(k, 2, NB):
                        pe.wait_ge(qk_ready, k + (n0 - 1))
                        wait_count(pe, qT_ready, k + (n0 - 2))
                        for i in range(2):
                            last = te.transpose(PS[:, 1, i * P:(i + 1) * P], qk[:, r, 2 * i, :], ident[:])
                        last.then_inc(q_turned, 1)
                        pe.wait_ge(v_copied, k + (n0 - 1))
                        wait_count(pe, kvd_ready, (k + (n0 - 2)) * 2)
                        for i in range(2):
                            last = te.matmul(KV, qk[:, r, 2 * i + 1, :], vext[:, r, i, :], start=(i == 0), stop=(i == 1))
                        last.then_inc(kv_done, 1)
                    if live(k, 3, NB):
                        pe.wait_ge(kvd_ready, (k + (n0 - 2)) * 2)
                        pe.wait_ge(qT_ready, k + (n0 - 2))
                        wait_count(pe, attn_done, k + (n0 - 3))
                        for i in range(2):
                            last = te.matmul(CTX[:, i, :], qT[:, s, i * P:(i + 1) * P], kvd[:, s, :],
                                             start=True, stop=True)
                        last.then_inc(ctx_done, 1)

                sweep(pe, 4, NB, 3, step)

            pe.wait_ge(const_step, NCONST)
            pe.wait_ge(small_loaded, 16 * NSMALL)
            for c in range(NCHUNK):
                route(c)
            pe.wait_ge(attn_loaded, 16 * NATTN)
            for n, (w, wf) in enumerate(((wq_s, wfq_s), (wk_s, wfk_s))):
                te.matmul(PS[:, 6, n * H:(n + 1) * H], w[:], wf[:], start=True, stop=True)
            for n, wf in enumerate((wfq_s, wfk_s)):
                last = te.matmul(PS[0:96, 7, n * H:(n + 1) * H], bqk_s[:, n:n + 1].broadcast_to([P, 96]), wf[:],
                                 start=True, stop=True)
            last.then_inc(fold_done, 1)
            pe.wait_ge(w_loaded, 16 * NW)
            pe.wait_ge(bias_ready, 2)
            for f in range(2):
                pe.wait_ge(route_done, (f + 1) * NCHUNK)
                for c in range(NCHUNK):
                    experts(f * NCHUNK + c)
                if f == 0:
                    pe.wait_ge(yrow_ready, NCHUNK * NG)
                    for c in range(NCHUNK):
                        if c:
                            pe.wait_ge(route_done, NCHUNK + c)
                        attention(c)
                        route(NCHUNK + c)


def kernel(L0_attn_hidden_states, L0_attn_Wq, L0_attn_bq, L0_attn_Wk, L0_attn_bk, L0_attn_Wv, L0_attn_bv,
           L0_attn_Wfq, L0_attn_bfq, L0_attn_Wfk, L0_attn_bfk, L0_ffn_norm_scale, L0_ffn_gate_w, L0_ffn_gate_b,
           L0_ffn_w1, L0_ffn_b1, L0_ffn_w2, L0_ffn_b2):
    import numpy as np
    import concourse.bacc as bacc
    from concourse.bass_utils import run_bass_kernel_spmd

    arr = {n: np.asarray(a) for n, a in (
        ("x", L0_attn_hidden_states), ("wq", L0_attn_Wq), ("bq", L0_attn_bq), ("wk", L0_attn_Wk), ("bk", L0_attn_bk),
        ("wv", L0_attn_Wv), ("bv", L0_attn_bv), ("wfq", L0_attn_Wfq), ("bfq", L0_attn_bfq), ("wfk", L0_attn_Wfk),
        ("bfk", L0_attn_bfk), ("nscale", L0_ffn_norm_scale), ("gw", L0_ffn_gate_w), ("gb", L0_ffn_gate_b),
        ("w1", L0_ffn_w1), ("b1", L0_ffn_b1), ("w2", L0_ffn_w2), ("b2", L0_ffn_b2))}
    w1 = arr["w1"].reshape(NE, H, 2, H)
    laid = [
        ("x", arr["x"].reshape(NTOK, H)),
        ("wq", arr["wq"]), ("bq", arr["bq"].reshape(H, 1)), ("wk", arr["wk"]), ("bk", arr["bk"].reshape(H, 1)),
        ("wvT", arr["wv"].T), ("bv", arr["bv"]), ("wfqT", arr["wfq"].T), ("bfq", arr["bfq"]),
        ("wfkT", arr["wfk"].T), ("bfk", arr["bfk"]),
        ("nscale", arr["nscale"].reshape(H, 1)), ("gwT", arr["gw"].T), ("gate_b", arr["gb"].reshape(1, NE)),
        ("w1T", w1.transpose(3, 0, 2, 1).reshape(H, NE * 2 * H)),
        ("b1", arr["b1"].reshape(NE, H, 2).transpose(0, 2, 1).reshape(NE, 2 * H)),
        ("w2T", arr["w2"].transpose(2, 0, 1).reshape(H, NE * H)), ("b2", arr["b2"]),
    ]
    nc = bacc.Bacc("TRN2", target_bir_lowering=False, num_devices=1)
    arrays, args = {}, []
    for name, a in laid:
        a = np.ascontiguousarray(a)
        arrays["in_" + name] = a
        args.append(nc.dram_tensor("in_" + name, a.shape, mybir.dt.from_np(a.dtype), kind="ExternalInput").ap())
    out = nc.dram_tensor("out", (NTOK, H), F32, kind="ExternalOutput").ap()
    xs = [nc.dram_tensor(f"xs{c}", (SLOTS, H), F32, kind="Internal").ap() for c in range(NCHUNK)]
    ys = [nc.dram_tensor(f"ys{c}", (SLOTS, H), F32, kind="Internal").ap() for c in range(NCHUNK)]
    build(nc, *args, out, xs, ys)
    r = run_bass_kernel_spmd(nc, [arrays], core_ids=[0])
    return r.results[0]["out"].reshape(16, 256, H)
```

```python
from contextlib import ExitStack

import concourse.bass as bass
from concourse import mybir


P = 128
H = 128
NTOK = 4096
NTILE = NTOK // P
NCHUNK = 2
CT = NTILE // NCHUNK
NE = 32
TOPK = 4
PAIRS = CT * TOPK
GT = 4
EW = 3 * H
ST = -(-(CT * TOPK + NE - 1) // (2 * GT)) * 2 * GT
NG = ST // GT
GW = GT * H
SLOTS = ST * P
NB = CT // 2
NHEAD = 16
HD = H // NHEAD
EPS = 1e-5
LIMIT = 7.0
NPHASE = 2 * NCHUNK
NRG = CT // GT
CG = 4
NCG = CT // CG
KVW = H + NHEAD
NGF = NCHUNK * NG
COMB0 = NGF - CT + 2
STORE_LAG = 5

ALU = mybir.AluOpType
ACT = mybir.ActivationFunctionType
F32 = mybir.dt.float32
BF16 = mybir.dt.bfloat16
I32 = mybir.dt.int32
U32 = mybir.dt.uint32
X_AXIS = mybir.AxisListType.X


def sweep(eng, lead, n, tail, body, cut=None, late=None):
    for k in range(lead):
        body(k, k % 2, k // 2)
    for first, stop, run in ((lead, cut or n, body), (cut or n, n, late)):
        if first < stop:
            with eng.Fori(0, (stop - first) // 2) as i:
                for r in range(2):
                    run(i * 2 + (first + r), r, i + first // 2)
    for k in range(n, n + tail):
        (late or body)(k, k % 2, k // 2)


def live(k, lag, n):
    return not isinstance(k, int) or 0 <= k - lag < n


def wait_count(eng, sem, count):
    if not isinstance(count, int) or count > 0:
        eng.wait_ge(sem, count)


def build(nc, x, wq, bq, wk, bk, wvT, bv, wfqT, bfq, wfkT, bfk,
          nscale, gwT, gate_b, w12T, b1, b2, out, xs, ys):
    with ExitStack() as ctx:
        def sb(name, shape, dt=F32):
            return ctx.enter_context(nc.sbuf_tensor(name, shape, dt))

        def sem(name):
            return ctx.enter_context(nc.semaphore(name))

        X = sb("X", [P, NTILE * H])
        U = sb("U", [P, NTILE * H])
        W = sb("W", [P, NE * EW])
        YG = sb("YG", [P, PAIRS, H])
        xrow = sb("xrow", [P, 2, GW])
        xT = sb("xT", [P, 2, GW])
        glulin = sb("glulin", [P, 2, 2, GW])
        glu, lin = glulin[:, 0], glulin[:, 1]
        swish = sb("swish", [P, 2, GW])
        hid = sb("hid", [P, 2, GW])
        hidT = sb("hidT", [P, 2, GW])
        yrow = sb("yrow", [P, 2, GW])
        ident = sb("ident", [P, P])
        before = sb("before", [P, P], BF16)
        ones = sb("ones", [P, P], BF16)
        parts_on = sb("parts_on", [96, P], BF16)
        expert_no = sb("expert_no", [P, NE], BF16)
        slot_no = sb("slot_no", [NE, ST])
        steps128 = sb("steps128", [NE, CT])
        ends = sb("ends", [NE, NE], BF16)
        starts128 = sb("starts128", [NE, NE], BF16)
        headblock = sb("headblock", [P, H])
        headcol = sb("headcol", [P, NHEAD])
        scale_col = sb("scale_col", [P, 1])
        gw = sb("gw", [P, NE])
        gb = sb("gb", [P, NE])
        bias_f = sb("bias_f", [96, 3 * H])
        bias_r = sb("bias_r", [96, 3 * H])
        bias_p = sb("bias_p", [96, 3 * H], BF16)
        bias3 = sb("bias3", [3, NE * EW], BF16)
        wq_s = sb("wq_s", [P, H])
        wk_s = sb("wk_s", [P, H])
        wfq_s = sb("wfq_s", [P, H])
        wfk_s = sb("wfk_s", [P, H])
        bqk_s = sb("bqk_s", [P, 2])
        qkvW = sb("qkvW", [P, 3 * H])
        abias_f = sb("abias_f", [96, 3 * H])
        abias_r = sb("abias_r", [96, 3 * H])
        abias_p = sb("abias_p", [96, 3 * H], BF16)
        st = sb("st", [P, CT * 6])
        sum2 = sb("sum2", [P, CT])
        dif = sb("dif", [P, CT])
        var = sb("var", [P, CT])
        vq = sb("vq", [P, 2 * CT])
        rs = sb("rs", [P, 2 * CT])
        nshift = sb("nshift", [P, CT])
        bscale = sb("bscale", [P, CT])
        bshift = sb("bshift", [P, CT])
        tT = xT
        logits = sb("logits", [P, CT * NE])
        top = sb("top", [P, CT * 8])
        topi = sb("topi", [P, CT * 8], U32)
        topf = sb("topf", [P, PAIRS], BF16)
        chosen = sb("chosen", [P, PAIRS * NE], BF16)
        place = glulin[:].rearrange("p a s n -> p (a s n)")
        mask = sb("mask", [P, CT * NE], BF16)
        counts = sb("counts", [NE, 1])
        over = sb("over", [NE, CT])
        ntiles = sb("ntiles", [NE, 1], BF16)
        span = sb("span", [NE, 1])
        ended = sb("ended", [NE, ST], BF16)
        eid = sb("eid", [1, NCHUNK * ST], I32)
        base = sb("base", [P, NE])
        where = sb("where", [P, CT * NE])
        pos = sb("pos", [P, PAIRS], I32)
        pos_a = sb("pos_a", [P, PAIRS], I32)
        pos_b = sb("pos_b", [P, PAIRS], I32)
        row = sb("row", [P, NCHUNK * PAIRS], I32)
        dlog = sb("dlog", [P, PAIRS])
        elog = sb("elog", [P, PAIRS])
        esum = sb("esum", [P, CT])
        erec = sb("erec", [P, CT])
        wtop = sb("wtop", [P, NCHUNK * PAIRS])
        arow = sb("arow", [P, 2, 2 * H])
        aT = hidT[:, 0].rearrange("p (s n) -> p s n", s=2)
        nmax = sb("nmax", [P, 2, 4])
        esm = swish[:].rearrange("p s (a h) -> p s a h", a=4)
        ssum = sb("ssum", [P, 2, 4])
        vext = sb("vext", [P, 2, 2, H + 2])
        qT = hidT[:, 1].rearrange("p (s n) -> p s n", s=2)
        kvd = sb("kvd", [P, 2, KVW])
        drec = sb("drec", [P, 2, NHEAD])
        ctxs = sb("ctxs", [P, 2, H])

        PS = ctx.enter_context(nc.psum_tensor("PS", [P, 8, 512], F32))
        TP = [PS[:, 0, :], PS[:, 1, :]]
        H1 = [PS[:, 2:4, :].rearrange("p a n -> p (a n)"), PS[:, 4:6, :].rearrange("p a n -> p (a n)")]
        HT = PS[:, 6, :]
        YP = PS[:, 7, :]
        LOG = [PS[:, 2, 0:GT * NE], PS[:, 5, 0:GT * NE]]
        RANK = PS[:, 3, :]
        CNT = PS[0:NE, 4, 0:1]
        SPAN = PS[0:NE, 4, 2:3]
        BASE = PS[:, 4, 4:4 + NE]
        EID = PS[0:1, 4, 64:64 + ST]
        KV = PS[:, 6, 0:H + 2]
        CTX = PS[:, 7, 0:2 * KVW].rearrange("p (a n) -> p a n", a=2)

        x_loaded = [sem(f"x_loaded{g}") for g in range(NRG)]
        x_rest_loaded = sem("x_rest_loaded")
        small_loaded = sem("small_loaded")
        attn_loaded = sem("attn_loaded")
        w_loaded = sem("w_loaded")
        zero_ready = sem("zero_ready")
        filled = [sem(f"filled{c}") for c in range(NCHUNK)]
        const_step = sem("const_step")
        chain = sem("chain")
        stats_done = sem("stats_done")
        var_ready = sem("var_ready")
        std_ready = sem("std_ready")
        norm_ready = sem("norm_ready")
        u_done = sem("u_done")
        base_done = sem("base_done")
        uT_done = sem("uT_done")
        tT_done = sem("tT_done")
        logits_done = sem("logits_done")
        logits_copied = sem("logits_copied")
        top_done = sem("top_done")
        topi_done = sem("topi_done")
        dlog_ready = sem("dlog_ready")
        elog_ready = sem("elog_ready")
        mask_ready = sem("mask_ready")
        counted = sem("counted")
        ntiles_ready = sem("ntiles_ready")
        spans_done = sem("spans_done")
        ended_ready = sem("ended_ready")
        eid_done = sem("eid_done")
        rows_ready = sem("rows_ready")
        route_done = sem("route_done")
        scattered = [sem(f"scattered{c}") for c in range(NCHUNK)]
        xrow_loaded = [sem(f"xrow_loaded{r}") for r in range(2)]
        x_turned = sem("x_turned")
        xT_ready = sem("xT_ready")
        h1_done = sem("h1_done")
        glu_ready = sem("glu_ready")
        lin_ready = sem("lin_ready")
        swish_ready = sem("swish_ready")
        hid_ready = sem("hid_ready")
        hid_turned = sem("hid_turned")
        hidT_ready = sem("hidT_ready")
        y_done = sem("y_done")
        yrow_ready = sem("yrow_ready")
        yrow_stored = [sem(f"yrow_stored{r}") for r in range(2)]
        gathered = [sem(f"gathered{r}") for r in range(2)]
        combined = sem("combined")
        fold_done = sem("fold_done")
        fold_copied = sem("fold_copied")
        bias_ready = sem("bias_ready")
        bias3_loaded = sem("bias3_loaded")
        arow_ready = sem("arow_ready")
        a_turned = sem("a_turned")
        aT_ready = sem("aT_ready")
        qkv_done = sem("qkv_done")
        nmax_ready = sem("nmax_ready")
        esm_ready = sem("esm_ready")
        v_copied = sem("v_copied")
        q_turned = sem("q_turned")
        qT_ready = sem("qT_ready")
        kv_done = sem("kv_done")
        kvd_ready = sem("kvd_ready")
        ctx_done = sem("ctx_done")
        drec_ready = sem("drec_ready")
        ctxs_ready = sem("ctxs_ready")
        srec_ready = sem("srec_ready")
        attn_done = sem("attn_done")
        based = sem("based")
        out_stored = sem("out_stored")

        x_v = x.rearrange("(c t p) h -> c p t h", c=NCHUNK, p=P)
        out_v = out.rearrange("(g t p) h -> g p t h", t=CG, p=P)
        xs_v = [a.rearrange("(g p q) h -> g p (q h)", p=P, q=GT) for a in xs]
        ys_v = [a.rearrange("(g p q) h -> g p (q h)", p=P, q=GT) for a in ys]
        zero = YG[:, 0:PAIRS // 2, :].rearrange("p a h -> p (a h)")
        ZW = PAIRS // 2 * H
        NZ = SLOTS * H // (P * ZW)
        assert NZ * P * ZW == SLOTS * H

        NSMALL, NATTN, NW = 3 + 6, 7 + 3, 1
        NCONST = 18

        block = ctx.enter_context(nc.Block())

        @block.sync
        def _(sp):
            for g in range(NRG):
                t = slice(g * GT, (g + 1) * GT)
                sp.dma_start(X[:, g * GW:(g + 1) * GW].rearrange("p (t h) -> p t h", h=H), x_v[0][:, t])\
                    .then_inc(x_loaded[g], 16)
            sp.dma_start(scale_col[:], nscale).then_inc(small_loaded, 16)
            sp.dma_start(gw[:], gwT).then_inc(small_loaded, 16)
            sp.dma_start(gb[:], gate_b.partition_broadcast(P)).then_inc(small_loaded, 16)
            for r in range(3):
                sp.dma_start(bias_f[NE * r:NE * r + NE, 0:2 * H], b1).then_inc(small_loaded, 16)
                sp.dma_start(bias_f[NE * r:NE * r + NE, 2 * H:3 * H], b2).then_inc(small_loaded, 16)
            sp.wait_ge(zero_ready, 1)
            for c in range(NCHUNK):
                for z in range(NZ):
                    sp.dma_start(xs[c].rearrange("(z p a) h -> z p (a h)", z=NZ, p=P)[z], zero)\
                        .then_inc(filled[c], 16)
                if c == 0:
                    for d in range(1, NCHUNK):
                        sp.dma_start(X[:, d * CT * H:(d + 1) * CT * H].rearrange("p (t h) -> p t h", h=H),
                                     x_v[d]).then_inc(x_rest_loaded, 16)
                    sp.dma_start(W[:], w12T).then_inc(w_loaded, 16)

            sp.wait_ge(bias_ready, 1)
            for q in range(3):
                sp.dma_start(bias3[q:q + 1, :].rearrange("o (e n) -> o e n", n=EW), bias_p[NE * q:NE * q + NE, :])\
                    .then_inc(bias3_loaded, 16)

            def experts(f):
                def load(c, k, r):
                    wait_count(sp, x_turned, k + (f * NGF + c * NG - 1))
                    sp.dma_start(xrow[:, r, :], xs_v[c][bass.ds(k, 1)].rearrange("g p n -> (g p) n"))\
                        .then_inc(xrow_loaded[r], 16)

                def store(c, k, r):
                    sp.wait_ge(yrow_ready, k + (f * NGF + c * NG + 1))
                    sp.dma_start(ys_v[c][bass.ds(k, 1)].rearrange("g p n -> (g p) n"), yrow[:, r, :])\
                        .then_inc(yrow_stored[r], 16)

                lead = STORE_LAG + 1
                for c in range(NCHUNK):
                    sp.wait_ge(scattered[c], 16 * PAIRS * (f + 1))
                    for k in range(lead):
                        load(c, k, k % 2)
                        if k >= STORE_LAG:
                            store(c, k - STORE_LAG, (k - STORE_LAG) % 2)
                        elif c:
                            store(c - 1, NG + k - STORE_LAG, (k - STORE_LAG) % 2)
                    with sp.Fori(0, (NG - lead) // 2) as i:
                        for r in range(2):
                            load(c, i * 2 + (lead + r), r)
                            store(c, i * 2 + (lead + r - STORE_LAG), (r + STORE_LAG) % 2)
                for k in range(NG - STORE_LAG, NG):
                    store(NCHUNK - 1, k, k % 2)

            for f in range(2):
                experts(f)
            for c in range(NCHUNK):
                for g in range(NCG):
                    sp.wait_ge(combined, PAIRS * (NCHUNK + c) + CG * TOPK * (g + 1))
                    t = c * CT + g * CG
                    sp.dma_start(out_v[c * NCG + g], X[:, t * H:(t + CG) * H].rearrange("p (t h) -> p t h", h=H))\
                        .then_inc(out_stored, 16)
            sp.wait_ge(out_stored, 16 * NCHUNK * NCG)

        @block.gpsimd
        def _(pool):
            made = [0]

            def step(ins):
                made[0] += 1
                ins.then_inc(const_step, 1)

            g = nc.gpsimd
            step(g.memset(ident[:], 0.0))
            step(g.memset(before[:], 1.0))
            step(g.memset(ends[:], 1.0))
            step(g.memset(starts128[:], 128.0))
            step(g.memset(headblock[:], 1.0))
            step(g.memset(headcol[:], 1.0))
            step(g.memset(ones[:], 1.0))
            step(g.iota(expert_no[:], [[1, NE]], base=0, channel_multiplier=0, allow_small_or_imprecise_dtypes=True))
            step(g.iota(slot_no[:], [[1, ST]], base=0, channel_multiplier=0, allow_small_or_imprecise_dtypes=True))
            step(g.iota(steps128[:], [[P, CT]], base=0, channel_multiplier=0, allow_small_or_imprecise_dtypes=True))
            pool.wait_ge(const_step, made[0])
            step(g.affine_select(out=ident[:], in_=ident[:], compare_op=ALU.not_equal, fill=1.0, base=0,
                                 pattern=[[-1, P]], channel_multiplier=1))
            step(g.affine_select(out=before[:], in_=before[:], compare_op=ALU.is_ge, fill=0.0, base=-1,
                                 pattern=[[1, P]], channel_multiplier=-1))
            step(g.affine_select(out=ends[:], in_=ends[:], compare_op=ALU.is_ge, fill=0.0,
                                 base=0, pattern=[[1, NE]], channel_multiplier=-1))
            step(g.affine_select(out=starts128[:], in_=starts128[:], compare_op=ALU.is_ge, fill=0.0,
                                 base=-1, pattern=[[1, NE]], channel_multiplier=-1))
            hb = headblock[:].rearrange("p (b d) -> p b d", d=HD)
            step(g.affine_select(out=hb, in_=hb, compare_op=ALU.is_ge, fill=0.0,
                                 base=0, pattern=[[-HD, NHEAD], [0, HD]], channel_multiplier=1))
            step(g.affine_select(out=headcol[:], in_=headcol[:], compare_op=ALU.is_ge, fill=0.0,
                                 base=0, pattern=[[-HD, NHEAD]], channel_multiplier=1))
            pool.wait_ge(const_step, made[0])
            step(g.affine_select(out=hb, in_=hb, compare_op=ALU.is_ge, fill=0.0,
                                 base=HD - 1, pattern=[[HD, NHEAD], [0, HD]], channel_multiplier=-1))
            step(g.affine_select(out=headcol[:], in_=headcol[:], compare_op=ALU.is_ge, fill=0.0,
                                 base=HD - 1, pattern=[[HD, NHEAD]], channel_multiplier=-1))
            assert made[0] == NCONST
            g.memset(YG[:, 0:PAIRS // 2, :], 0.0).then_inc(zero_ready, 1)

            def scatter(ph):
                c = ph % NCHUNK
                pool.wait_ge(u_done, CT * (ph + 1))
                pool.wait_ge(rows_ready, 2 * ph + 1)
                if ph < NCHUNK:
                    pool.wait_ge(filled[c], 16 * NZ)
                for t in range(CT):
                    if t == GT:
                        pool.wait_ge(rows_ready, 2 * ph + 2)
                    for k in range(TOPK):
                        i = c * PAIRS + t * TOPK + k
                        pool.indirect_dma_start(
                            out=xs[c], out_offset=bass.IndirectOffsetOnAxis(ap=row[:, i:i + 1], axis=0),
                            in_=U[:, (c * CT + t) * H:(c * CT + t + 1) * H], in_offset=None,
                        ).then_inc(scattered[c], 16)

            def gather(ph):
                c = ph % NCHUNK
                for r in range(2):
                    pool.wait_ge(yrow_stored[r], 16 * (NG // 2) * (ph + 1))
                if ph == 0:
                    for d in range(NCHUNK):
                        pool.wait_ge(filled[d], 16 * NZ)
                for t in range(CT):
                    if ph and t % CG == 0:
                        pool.wait_ge(combined, PAIRS * (ph - 1) + TOPK * (t + CG))
                    wait_count(pool, gathered[t % 2], 16 * TOPK * ((ph * CT + t) // 2))
                    for k in range(TOPK):
                        i = c * PAIRS + t * TOPK + k
                        pool.indirect_dma_start(
                            out=YG[:, t * TOPK + k, :], out_offset=None,
                            in_=ys[c], in_offset=bass.IndirectOffsetOnAxis(ap=row[:, i:i + 1], axis=0),
                        ).then_inc(gathered[t % 2], 16)

            for f in range(2):
                for c in range(NCHUNK):
                    scatter(f * NCHUNK + c)
                for c in range(NCHUNK):
                    gather(f * NCHUNK + c)

        @block.scalar
        def _(act):
            a = nc.scalar
            for dst, src in ((wq_s, wq), (wk_s, wk), (wfq_s, wfqT), (wfk_s, wfkT)):
                act.dma_start(dst[:], src).then_inc(attn_loaded, 16)
            act.dma_start(qkvW[:, 2 * H:3 * H], wvT).then_inc(attn_loaded, 16)
            act.dma_start(bqk_s[:, 0:1], bq).then_inc(attn_loaded, 16)
            act.dma_start(bqk_s[:, 1:2], bk).then_inc(attn_loaded, 16)
            for n, src in enumerate((bfq, bfk, bv)):
                act.dma_start(abias_f[:, n * H:(n + 1) * H], src.partition_broadcast(96)).then_inc(attn_loaded, 16)

            def normalise(n):
                act.wait_ge(var_ready, n + 1)
                a.activation(vq[:], vq[:], ACT.Sqrt).then_inc(std_ready, 1)

            def route(ph, n):
                c = ph % NCHUNK
                normalise(n)
                act.wait_ge(norm_ready, n + 1)
                if ph >= NCHUNK:
                    act.wait_ge(scattered[c], 16 * PAIRS * (ph // NCHUNK))

                def rows(q):
                    for t in range(q * GT, (q + 1) * GT):
                        i = (c * CT + t) * H
                        a.activation(U[:, i:i + H], X[:, i:i + H], ACT.Identity, scale=rs[:, CT + t:CT + t + 1],
                                     bias=nshift[:, t:t + 1]).then_inc(u_done, 1)

                rows(0)
                if ph == 0:
                    act.wait_ge(small_loaded, 16 * NSMALL)
                for q in range(NRG):
                    if q + 1 < NRG:
                        rows(q + 1)
                    Q = ph * NRG + q
                    act.wait_ge(uT_done, Q + 1)
                    wait_count(act, logits_done, Q - 1)
                    a.activation(tT[:, q % 2, :], TP[q % 2], ACT.Copy, scale=scale_col[:, 0:1]).then_inc(tT_done, 1)
                act.wait_ge(dlog_ready, ph + 1)
                a.activation(elog[:], dlog[:], ACT.Exp).then_inc(elog_ready, 1)

            def experts(f):
                g0 = f * NGF

                def step(k, r, m):
                    s = 1 - r
                    if live(k, 0, NGF):
                        act.wait_ge(x_turned, k + (g0 + 1))
                        wait_count(act, h1_done, k + (g0 - 1))
                        a.activation(xT[:, r, :], TP[r], ACT.Copy, scale=scale_col[:, 0:1]).then_inc(xT_ready, 1)
                    if live(k, 3, NGF):
                        act.wait_ge(hid_turned, k + (g0 - 2))
                        wait_count(act, y_done, k + (g0 - 4))
                        a.activation(hidT[:, s, :], HT, ACT.Copy).then_inc(hidT_ready, 1)
                    if live(k, 1, NGF):
                        act.wait_ge(glu_ready, k + g0)
                        wait_count(act, hid_ready, k + (g0 - 2))
                        a.activation(swish[:, s, :], glu[:, s, :], ACT.Gelu_apprx_sigmoid).then_inc(swish_ready, 1)

                sweep(act, 6, NGF, 3, step)

            def attention(c, n):
                n0 = c * NB
                normalise(n)
                act.wait_ge(norm_ready, n + 1)

                def norm_rows(k, s):
                    wait_count(act, a_turned, k + (n0 - 1))
                    for i in range(2):
                        t = k * 2 + i
                        a.activation(arow[:, s, i * H:(i + 1) * H], X[:, bass.ds((t + c * CT) * H, H)], ACT.Identity,
                                     scale=rs[:, bass.ds(t, 1)], bias=nshift[:, bass.ds(t, 1)]).then_inc(arow_ready, 1)

                def step(k, r, m):
                    s = 1 - r
                    if live(k, 0, NB):
                        act.wait_ge(a_turned, k + (n0 + 1))
                        wait_count(act, qkv_done, k + (n0 - 1))
                        a.activation(aT[:, r, :], PS[:, 0, 0:2 * H], ACT.Copy).then_inc(aT_ready, 1)
                    if live(k, -1, NB):
                        norm_rows(k + 1, s)
                    if live(k, 1, NB):
                        act.wait_ge(nmax_ready, k + n0)
                        wait_count(act, kv_done, k + (n0 - 2))
                        for i in range(4):
                            a.activation(esm[:, s, i, :], PS[:, 2 + 2 * s + i // 2, (i % 2) * H:(i % 2 + 1) * H], ACT.Exp,
                                         bias=nmax[:, s, i:i + 1], accum_out=ssum[:, s, i:i + 1]).then_inc(esm_ready, 1)
                    if live(k, 2, NB):
                        act.wait_ge(q_turned, k + (n0 - 1))
                        wait_count(act, ctx_done, k + (n0 - 3))
                        a.activation(qT[:, r, :], PS[:, 1, 0:2 * H], ACT.Copy).then_inc(qT_ready, 1)
                    if live(k, 1, NB):
                        act.wait_ge(srec_ready, k + n0)
                        for i in range(2):
                            a.activation(vext[:, s, i, 0:H], PS[:, 2 + 2 * s + i, 2 * H:3 * H], ACT.Copy,
                                         scale=vext[:, s, i, H:H + 1]).then_inc(v_copied, 1)

                norm_rows(0, 0)
                sweep(act, 4, NB - 2, 5, step)

            for c in range(NCHUNK):
                route(c, c)
            experts(0)
            for c in range(NCHUNK):
                attention(c, NCHUNK + 2 * c)
                route(NCHUNK + c, NCHUNK + 2 * c + 1)
            experts(1)

        @block.vector
        def _(dve):
            v = nc.vector
            linked = [0]

            def link(ins):
                linked[0] += 1
                ins.then_inc(chain, 1)
                dve.wait_ge(chain, linked[0])

            def stats(t, tile):
                v.bn_stats(st[:, bass.ds(tile * 6, 6)], X[:, bass.ds(t * H, H)]).then_inc(stats_done, 1)

            def normalise(n, rows):
                dve.wait_ge(stats_done, CT * (n + 1))
                s6 = st[:].rearrange("p (t s) -> p s t", s=6)
                link(v.tensor_tensor(sum2[:], s6[:, 1, :], s6[:, 4, :], ALU.add))
                link(v.tensor_tensor(dif[:], s6[:, 1, :], s6[:, 4, :], ALU.subtract))
                link(v.tensor_tensor(var[:], s6[:, 2, :], s6[:, 5, :], ALU.add))
                link(v.scalar_tensor_tensor(dif[:], dif[:], 0.25, dif[:], ALU.mult, ALU.mult))
                link(v.scalar_tensor_tensor(var[:], var[:], 1.0 / H, dif[:], ALU.mult, ALU.add))
                link(v.tensor_scalar(vq[:, 0:CT], var[:], EPS, None, ALU.add))
                v.scalar_tensor_tensor(vq[:, CT:2 * CT], vq[:, 0:CT], EPS, var[:], ALU.mult, ALU.add)\
                    .then_inc(var_ready, 1)
                dve.wait_ge(std_ready, n + 1)
                link(v.reciprocal(rs[:], vq[:]))
                v.scalar_tensor_tensor(nshift[:], sum2[:], -0.5, rs[:, rows], ALU.mult, ALU.mult)\
                    .then_inc(norm_ready, 1)

            def route(ph, n):
                c = ph % NCHUNK
                normalise(n, slice(CT, 2 * CT))
                link(v.tensor_scalar(bscale[:], rs[:, 0:CT], 0.5, 1.0, ALU.mult, ALU.add))
                link(v.scalar_tensor_tensor(bshift[:], sum2[:], -0.25, rs[:, 0:CT], ALU.mult, ALU.mult))

                def residual(q):
                    dve.wait_ge(u_done, CT * ph + (q + 1) * GT)
                    for t in range(q * GT, (q + 1) * GT):
                        xt = X[:, (c * CT + t) * H:(c * CT + t + 1) * H]
                        v.tensor_scalar(xt, xt, bscale[:, t:t + 1], bshift[:, t:t + 1],
                                        ALU.mult, ALU.add).then_inc(base_done, 1)

                residual(0)
                residual(1)
                if ph == 0:
                    dve.wait_ge(small_loaded, 16 * NSMALL)
                for q in range(NRG):
                    Q = ph * NRG + q
                    tiles = range(q * GT, (q + 1) * GT)
                    dve.wait_ge(logits_done, Q + 1)
                    v.tensor_tensor(logits[:, q * GT * NE:(q + 1) * GT * NE].rearrange("p (t e) -> p t e", e=NE),
                                    LOG[q % 2].rearrange("p (t e) -> p t e", e=NE),
                                    gb[:].rearrange("p (o e) -> p o e", o=1).broadcast_to([P, GT, NE]), ALU.add)\
                        .then_inc(logits_copied, 1)
                    dve.wait_ge(logits_copied, Q + 1)
                    for t in tiles:
                        v.max(top[:, t * 8:t * 8 + 8], logits[:, t * NE:(t + 1) * NE]).then_inc(top_done, 1)
                    for t in tiles:
                        dve.wait_ge(top_done, CT * ph + t + 1)
                        v.max_index(topi[:, t * 8:t * 8 + 8], top[:, t * 8:t * 8 + 8], logits[:, t * NE:(t + 1) * NE])\
                            .then_inc(topi_done, 1)
                    dve.wait_ge(topi_done, CT * ph + (q + 1) * GT)
                    tf = topf[:, q * GT * TOPK:(q + 1) * GT * TOPK]
                    link(v.tensor_copy(tf.rearrange("p (t k) -> p t k", k=TOPK),
                                       topi[:, q * GT * 8:(q + 1) * GT * 8].rearrange("p (t k) -> p t k", k=8)[:, :, 0:TOPK]))
                    ch = chosen[:, q * GT * TOPK * NE:(q + 1) * GT * TOPK * NE]
                    link(v.tensor_tensor(ch.rearrange("p (t e) -> p t e", e=NE),
                                         expert_no[:].rearrange("p (o e) -> p o e", o=1).broadcast_to([P, GT * TOPK, NE]),
                                         tf.rearrange("p (t o) -> p t o", o=1).broadcast_to([P, GT * TOPK, NE]),
                                         ALU.is_equal))
                    with nc.allow_low_precision(reason="sums of at most one 1"):
                        v.tensor_reduce(mask[:, q * GT * NE:(q + 1) * GT * NE].rearrange("p (t e) -> p t e", e=NE),
                                        ch.rearrange("p (t k e) -> p t e k", k=TOPK, e=NE), X_AXIS, ALU.add)\
                            .then_inc(mask_ready, 1)
                t8 = top[:].rearrange("p (t k) -> p t k", k=8)
                tk = [P, CT, TOPK]
                v.tensor_tensor(dlog[:].rearrange("p (t k) -> p t k", k=TOPK), t8[:, :, 0:TOPK],
                                t8[:, :, 0:1].broadcast_to(tk), ALU.subtract).then_inc(dlog_ready, 1)
                dve.wait_ge(counted, ph + 1)
                link(v.tensor_copy(counts[:], CNT))
                link(v.tensor_scalar(over[:], steps128[:], counts[:, 0:1], None, ALU.is_lt))
                with nc.allow_low_precision(reason="integers up to 16"):
                    v.tensor_reduce(ntiles[:], over[:], X_AXIS, ALU.add).then_inc(ntiles_ready, 1)
                dve.wait_ge(spans_done, ph + 1)
                v.tensor_copy(base[:], BASE).then_inc(based, 1)
                v.tensor_copy(span[:], SPAN).then_inc(based, 1)
                dve.wait_ge(based, 2 * ph + 2)

                def rows(first, stop):
                    n = stop - first
                    wh = where[:, first * NE:stop * NE].rearrange("p (t e) -> p t e", e=NE)
                    pr = slice(first * TOPK, stop * TOPK)
                    ch = chosen[:, first * TOPK * NE:stop * TOPK * NE]
                    pl = place[:, first * TOPK * NE:stop * TOPK * NE]
                    link(v.tensor_tensor(wh, RANK[:, first * NE:stop * NE].rearrange("p (t e) -> p t e", e=NE),
                                         base[:].rearrange("p (o e) -> p o e", o=1).broadcast_to([P, n, NE]), ALU.add))
                    link(v.tensor_tensor(pl.rearrange("p (t k e) -> p t k e", k=TOPK, e=NE),
                                         ch.rearrange("p (t k e) -> p t k e", k=TOPK, e=NE),
                                         where[:, first * NE:stop * NE].rearrange("p (t o e) -> p t o e", o=1, e=NE)
                                         .broadcast_to([P, n, TOPK, NE]), ALU.mult))
                    with nc.allow_low_precision(reason="one integer and zeros"):
                        link(v.tensor_reduce(pos[:, pr], pl.rearrange("p (t e) -> p t e", e=NE), X_AXIS, ALU.add))
                    link(v.tensor_scalar(pos_a[:, pr], pos[:, pr], P - 1, 2, ALU.bitwise_and, ALU.logical_shift_left))
                    link(v.tensor_scalar(pos_b[:, pr], pos[:, pr], 7, GT - 1, ALU.logical_shift_right, ALU.bitwise_and))
                    link(v.tensor_tensor(pos_a[:, pr], pos_a[:, pr], pos_b[:, pr], ALU.bitwise_or))
                    link(v.tensor_scalar(pos_b[:, pr], pos[:, pr], 9, 9, ALU.logical_shift_right, ALU.logical_shift_left))
                    v.tensor_tensor(row[:, c * PAIRS + first * TOPK:c * PAIRS + stop * TOPK], pos_a[:, pr], pos_b[:, pr],
                                    ALU.bitwise_or).then_inc(rows_ready, 1)

                rows(0, GT)
                v.tensor_scalar(ended[:], slot_no[:], span[:, 0:1], None, ALU.is_ge).then_inc(ended_ready, 1)
                rows(GT, CT)
                dve.wait_ge(eid_done, ph + 1)
                v.tensor_scalar(eid[:, c * ST:(c + 1) * ST], EID, float(NE - 1), float(EW), ALU.min, ALU.mult)\
                    .then_inc(route_done, 1)
                dve.wait_ge(elog_ready, ph + 1)
                el = elog[:].rearrange("p (t k) -> p t k", k=TOPK)
                link(v.tensor_reduce(esum[:], el, X_AXIS, ALU.add))
                link(v.reciprocal(erec[:], esum[:]))
                link(v.scalar_tensor_tensor(wtop[:, c * PAIRS:(c + 1) * PAIRS].rearrange("p (t k) -> p t k", k=TOPK), el,
                                            0.5, erec[:].rearrange("p (t o) -> p t o", o=1).broadcast_to(tk),
                                            ALU.mult, ALU.mult))
                residual(2)
                residual(3)

            def split(src, rest, dst):
                link(v.tensor_copy(dst[:], src[:]))
                link(v.tensor_tensor(rest[:], src[:], dst[:], ALU.subtract))
                for q in (1, 2):
                    link(v.tensor_copy(dst[NE * q:NE * q + NE, :], rest[NE * q:NE * q + NE, :]))
                link(v.tensor_tensor(rest[64:96, :], rest[64:96, :], dst[64:96, :], ALU.subtract))
                v.tensor_copy(dst[64:96, :], rest[64:96, :]).then_inc(bias_ready, 1)

            def experts(f):
                g0, ph = f * NGF, f * NCHUNK

                def step(k, r, m, combining=False):
                    s = 1 - r
                    h1 = H1[s].rearrange("p (q g f) -> p g q f", q=GT, g=2)
                    t = k - COMB0
                    adding = combining and live(t, 0, CT)

                    def add(j):
                        if not adding:
                            return
                        if j == 0:
                            dve.wait_ge(gathered[r], (m + (ph * CT - COMB0) // 2 + 1) * (16 * TOPK))
                        else:
                            dve.wait_ge(combined, t * TOPK + (PAIRS * ph + j))
                        xt = X[:, bass.ds(t * H, H)]
                        v.scalar_tensor_tensor(xt, YG[:, bass.ds(t * TOPK + j, 1), :].rearrange("p o h -> p (o h)"),
                                               wtop[:, bass.ds(t * TOPK + j, 1)], xt, ALU.mult, ALU.add)\
                            .then_inc(combined, 1)

                    if live(k, 4, NGF):
                        dve.wait_ge(y_done, k + (g0 - 3))
                        wait_count(dve, yrow_stored[r], (m + (g0 // 2 - 2)) * 16)
                        v.tensor_copy(yrow[:, r, :], YP).then_inc(yrow_ready, 1)
                    add(0)
                    if live(k, 1, NGF):
                        dve.wait_ge(h1_done, k + g0)
                        wait_count(dve, swish_ready, k + (g0 - 2))
                        v.tensor_scalar(glu[:, s, :].rearrange("p (q f) -> p q f", q=GT), h1[:, 0],
                                        LIMIT, None, ALU.min).then_inc(glu_ready, 1)
                    add(1)
                    if live(k, 1, NGF):
                        wait_count(dve, hid_ready, k + (g0 - 2))
                        v.tensor_scalar(lin[:, s, :].rearrange("p (q f) -> p q f", q=GT), h1[:, 1],
                                        -LIMIT, LIMIT, ALU.max, ALU.min).then_inc(lin_ready, 1)
                    add(2)
                    if live(k, 1, NGF):
                        dve.wait_ge(swish_ready, k + g0)
                        dve.wait_ge(lin_ready, k + g0)
                        wait_count(dve, hid_turned, k + (g0 - 2))
                        v.scalar_tensor_tensor(hid[:, s, :], lin[:, s, :], 1.0, swish[:, s, :], ALU.add, ALU.mult)\
                            .then_inc(hid_ready, 1)
                    add(3)
                    if adding and f == 0:
                        dve.wait_ge(combined, t * TOPK + (PAIRS * ph + TOPK))
                        stats(t, t)

                dve.wait_ge(base_done, CT * (ph + 1))
                sweep(dve, 6, NGF, 4, step, COMB0, lambda k, r, m: step(k, r, m, True))

            def combine(ph):
                c = ph % NCHUNK
                dve.wait_ge(base_done, CT * (ph + 1))
                for g in range(NCG):
                    tiles = range(g * CG, g * CG + CG)
                    for r in range(2):
                        dve.wait_ge(gathered[r], 16 * TOPK * ((ph * CT + (g + 1) * CG) // 2))
                    for k in range(TOPK):
                        for t in tiles:
                            if k:
                                dve.wait_ge(combined, PAIRS * ph + CG * TOPK * g + CG * (k - 1) + t % CG + 1)
                            xt = X[:, (c * CT + t) * H:(c * CT + t + 1) * H]
                            w = c * PAIRS + t * TOPK + k
                            v.scalar_tensor_tensor(xt, YG[:, t * TOPK + k, :], wtop[:, w:w + 1], xt,
                                                   ALU.mult, ALU.add).then_inc(combined, 1)
                    if ph < NCHUNK:
                        for t in tiles:
                            dve.wait_ge(combined, PAIRS * ph + CG * TOPK * (g + 1) - CG + t % CG + 1)
                            stats(c * CT + t, t)

            def attention(c, n):
                n0 = c * NB
                normalise(n, slice(0, CT))

                def step(k, r, m):
                    s = 1 - r
                    if live(k, 1, NB):
                        dve.wait_ge(qkv_done, k + n0)
                        v.tensor_reduce(nmax[:, s, :].rearrange("p (a b) -> p a b", a=2),
                                        PS[:, 2 + 2 * s:4 + 2 * s, 0:2 * H].rearrange("p a (b h) -> p a b h", b=2),
                                        X_AXIS, ALU.max, negate=True).then_inc(nmax_ready, 1)
                    if live(k, 2, NB):
                        dve.wait_ge(kv_done, k + (n0 - 1))
                        wait_count(dve, ctx_done, k + (n0 - 3))
                        v.tensor_tensor(kvd[:, r, 0:H], KV[:, 0:H], headblock[:], ALU.mult).then_inc(kvd_ready, 1)
                        v.tensor_tensor(kvd[:, r, H:KVW], headcol[:], KV[:, H:H + 1].broadcast_to([P, NHEAD]),
                                        ALU.mult).then_inc(kvd_ready, 1)
                    if live(k, 1, NB):
                        dve.wait_ge(esm_ready, (k + n0) * 4)
                        wait_count(dve, kv_done, k + (n0 - 2))
                        v.reciprocal(vext[:, s, :, H:H + 1],
                                     ssum[:, s, :].rearrange("p (a b) -> p a b", b=2)[:, :, 1:2]).then_inc(srec_ready, 1)
                    if live(k, 3, NB):
                        dve.wait_ge(ctx_done, k + (n0 - 2))
                        v.reciprocal(drec[:], CTX[:, :, H:KVW]).then_inc(drec_ready, 1)
                        dve.wait_ge(drec_ready, k + (n0 - 2))
                        v.tensor_tensor(ctxs[:].rearrange("p a (h d) -> p a h d", d=HD),
                                        CTX[:, :, 0:H].rearrange("p a (h d) -> p a h d", d=HD),
                                        drec[:].rearrange("p a (h o) -> p a h o", o=1).broadcast_to([P, 2, NHEAD, HD]),
                                        ALU.mult).then_inc(ctxs_ready, 1)
                        dve.wait_ge(ctxs_ready, k + (n0 - 2))
                        xt = X[:, bass.ds((k - 3) * (2 * H) + c * CT * H, 2 * H)]
                        v.tensor_tensor(xt, xt, ctxs[:].rearrange("p a n -> p (a n)"), ALU.add).then_inc(attn_done, 1)
                        for i in range(2):
                            t = (k - 3) * 2 + i
                            dve.wait_ge(attn_done, k + (n0 - 2))
                            stats(t + c * CT, t)

                sweep(dve, 4, NB, 3, step)
                dve.wait_ge(attn_done, n0 + NB)

            dve.wait_ge(const_step, NCONST)
            for c in range(NCHUNK):
                for t in range(CT):
                    if c:
                        dve.wait_ge(x_rest_loaded, 16 * (NCHUNK - 1))
                    elif t % GT == 0:
                        dve.wait_ge(x_loaded[t // GT], 16)
                    stats(c * CT + t, t)
                route(c, c)
                if c == 0:
                    split(bias_f, bias_r, bias_p)
            link(v.memset(parts_on[:], 0.0))
            for r in range(3):
                link(v.memset(parts_on[NE * r:NE * r + 1, :], 1.0))
            for s in range(2):
                link(v.memset(vext[:, s, :, H:H + 2], 1.0))
            dve.wait_ge(fold_done, 1)
            dve.wait_ge(attn_loaded, 16 * NATTN)
            v.tensor_copy(qkvW[:, 0:2 * H], PS[:, 6, 0:2 * H]).then_inc(fold_copied, 1)
            link(v.tensor_tensor(abias_f[:, 0:2 * H], abias_f[:, 0:2 * H], PS[0:96, 7, 0:2 * H], ALU.add))
            split(abias_f, abias_r, abias_p)
            experts(0)
            for c in range(NCHUNK):
                if c:
                    combine(c)
                attention(c, NCHUNK + 2 * c)
                route(NCHUNK + c, NCHUNK + 2 * c + 1)
            experts(1)
            combine(NPHASE - 1)

        @block.tensor
        def _(pe):
            te = nc.tensor

            def turn(dst, src, n):
                for q in range(n):
                    last = te.transpose(dst[:, q * P:(q + 1) * P], src[:, q * H:(q + 1) * H], ident[:])
                return last

            def route(ph):
                c = ph % NCHUNK

                def turned(q):
                    pe.wait_ge(u_done, CT * ph + (q + 1) * GT)
                    wait_count(pe, tT_done, ph * NRG + q - 1)
                    t0 = (c * CT + q * GT) * H
                    turn(TP[q % 2], U[:, t0:t0 + GW], GT).then_inc(uT_done, 1)

                def scores(q):
                    pe.wait_ge(tT_done, ph * NRG + q + 1)
                    wait_count(pe, logits_copied, ph * NRG + q - 1)
                    for i in range(GT):
                        last = te.matmul(LOG[q % 2][:, i * NE:(i + 1) * NE], tT[:, q % 2, i * P:(i + 1) * P], gw[:],
                                         start=True, stop=True)
                    last.then_inc(logits_done, 1)

                def rank(q):
                    pe.wait_ge(mask_ready, ph * NRG + q + 1)
                    if q == 0:
                        wait_count(pe, route_done, ph)
                    for i in range(q * GT, (q + 1) * GT):
                        m = mask[:, i * NE:(i + 1) * NE]
                        n = CT - 1 - i
                        te.matmul(RANK[:, i * NE:(i + 1) * NE], before[:], m, start=(i == 0), stop=(i in (0, CT - 1)))
                        if n:
                            te.matmul(RANK[:, (i + 1) * NE:CT * NE].rearrange("p (t e) -> p t e", e=NE), ones[:],
                                      m.rearrange("p (o e) -> p o e", o=1).broadcast_to([P, n, NE]),
                                      start=(i == 0), stop=False)
                        last = te.matmul(CNT, m, ones[:, 0:1], start=(i == 0), stop=(i == CT - 1))
                    return last

                turned(0)
                for q in range(NRG):
                    if q + 1 < NRG:
                        turned(q + 1)
                    scores(q)
                    if q >= 2:
                        rank(q - 2)
                rank(NRG - 2)
                rank(NRG - 1).then_inc(counted, 1)
                pe.wait_ge(ntiles_ready, ph + 1)
                te.matmul(SPAN, ends[:], ntiles[:], start=True, stop=True)
                te.matmul(BASE, ntiles[:, 0:1].broadcast_to([NE, P]), starts128[:], start=True, stop=True)\
                    .then_inc(spans_done, 1)
                pe.wait_ge(ended_ready, ph + 1)
                pe.wait_ge(based, 2 * ph + 2)
                te.matmul(EID, ones[0:NE, 0:1], ended[:], start=True, stop=True).then_inc(eid_done, 1)

            def experts(f):
                g0 = f * NGF

                def experts_of(g):
                    _, es = nc.values_load_multi_w_load_instructions(
                        eid[0:1, bass.ds(g * GT, GT)], engines=[te.engine], min_val=0, max_val=(NE - 1) * EW,
                        skip_runtime_bounds_check_because="the router cuts them to NE - 1 times EW")
                    return es

                def step(k, r, m):
                    s = 1 - r
                    if live(k, 0, NGF):
                        pe.wait_ge(xrow_loaded[r], (m + (g0 // 2 + 1)) * 16)
                        wait_count(pe, xT_ready, k + (g0 - 1))
                        turn(TP[r], xrow[:, r, :], GT).then_inc(x_turned, 1)
                    if live(k, 3, NGF):
                        pe.wait_ge(hid_ready, k + (g0 - 2))
                        wait_count(pe, hidT_ready, k + (g0 - 3))
                        turn(HT, hid[:, s, :], GT).then_inc(hid_turned, 1)
                    if live(k, 1, NGF):
                        es = experts_of(k - 1)
                        pe.wait_ge(xT_ready, k + g0)
                        wait_count(pe, glu_ready, k + (g0 - 2))
                        wait_count(pe, lin_ready, k + (g0 - 2))
                        for q in range(GT):
                            h1 = H1[s][:, q * 2 * H:(q + 1) * 2 * H]
                            te.matmul(h1, ones[0:3, :], bias3[:, bass.ds(es[q], 2 * H)], start=True, stop=False)
                            last = te.matmul(h1, xT[:, s, q * P:(q + 1) * P], W[:, bass.ds(es[q], 2 * H)],
                                             start=False, stop=True)
                        last.then_inc(h1_done, 1)
                    if live(k, 3, NGF):
                        es = experts_of(k - 3)
                        pe.wait_ge(hidT_ready, k + (g0 - 2))
                        wait_count(pe, yrow_ready, k + (g0 - 3))
                        for q in range(GT):
                            y = YP[:, q * H:(q + 1) * H]
                            te.matmul(y, ones[0:3, :], bias3[:, bass.ds(es[q] + 2 * H, H)], start=True, stop=False)
                            last = te.matmul(y, hidT[:, s, q * P:(q + 1) * P], W[:, bass.ds(es[q] + 2 * H, H)],
                                             start=False, stop=True)
                        last.then_inc(y_done, 1)

                sweep(pe, 4, NGF, 3, step)

            def attention(c):
                n0 = c * NB

                def step(k, r, m):
                    s = 1 - r
                    if live(k, 0, NB):
                        pe.wait_ge(arow_ready, (k + (n0 + 1)) * 2)
                        wait_count(pe, aT_ready, k + n0)
                        turn(PS[:, 0, :], arow[:, r, :], 2).then_inc(a_turned, 1)
                    if live(k, 1, NB):
                        pe.wait_ge(aT_ready, k + n0)
                        wait_count(pe, v_copied, (k + (n0 - 2)) * 2)
                        for i in range(2):
                            o = PS[:, 2 + 2 * s + i, 0:3 * H]
                            te.matmul(o, parts_on[:], abias_p[:], start=True, stop=False)
                            last = te.matmul(o, aT[:, s, i * P:(i + 1) * P], qkvW[:], start=False, stop=True)
                        last.then_inc(qkv_done, 1)
                    if live(k, 2, NB):
                        pe.wait_ge(esm_ready, (k + (n0 - 1)) * 4)
                        wait_count(pe, qT_ready, k + (n0 - 2))
                        for i in range(2):
                            last = te.transpose(PS[:, 1, i * P:(i + 1) * P], esm[:, r, 2 * i, :], ident[:])
                        last.then_inc(q_turned, 1)
                        pe.wait_ge(v_copied, (k + (n0 - 1)) * 2)
                        wait_count(pe, kvd_ready, (k + (n0 - 2)) * 2)
                        for i in range(2):
                            last = te.matmul(KV, esm[:, r, 2 * i + 1, :], vext[:, r, i, :], start=(i == 0), stop=(i == 1))
                        last.then_inc(kv_done, 1)
                    if live(k, 3, NB):
                        pe.wait_ge(kvd_ready, (k + (n0 - 2)) * 2)
                        pe.wait_ge(qT_ready, k + (n0 - 2))
                        wait_count(pe, attn_done, k + (n0 - 3))
                        for i in range(2):
                            last = te.matmul(CTX[:, i, :], qT[:, s, i * P:(i + 1) * P], kvd[:, s, :],
                                             start=True, stop=True)
                        last.then_inc(ctx_done, 1)

                sweep(pe, 4, NB, 3, step)

            pe.wait_ge(const_step, NCONST)
            pe.wait_ge(small_loaded, 16 * NSMALL)
            for c in range(NCHUNK):
                route(c)
            pe.wait_ge(attn_loaded, 16 * NATTN)
            for n, (w, wf) in enumerate(((wq_s, wfq_s), (wk_s, wfk_s))):
                te.matmul(PS[:, 6, n * H:(n + 1) * H], w[:], wf[:], start=True, stop=True)
            for n, wf in enumerate((wfq_s, wfk_s)):
                last = te.matmul(PS[0:96, 7, n * H:(n + 1) * H], bqk_s[:, n:n + 1].broadcast_to([P, 96]), wf[:],
                                 start=True, stop=True)
            last.then_inc(fold_done, 1)
            pe.wait_ge(w_loaded, 16 * NW)
            pe.wait_ge(bias3_loaded, 16 * 3)
            pe.wait_ge(bias_ready, 2)
            for f in range(2):
                pe.wait_ge(route_done, (f + 1) * NCHUNK)
                experts(f)
                if f == 0:
                    pe.wait_ge(yrow_ready, NGF)
                    for c in range(NCHUNK):
                        if c:
                            pe.wait_ge(route_done, NCHUNK + c)
                        attention(c)
                        route(NCHUNK + c)


def kernel(L0_attn_hidden_states, L0_attn_Wq, L0_attn_bq, L0_attn_Wk, L0_attn_bk, L0_attn_Wv, L0_attn_bv,
           L0_attn_Wfq, L0_attn_bfq, L0_attn_Wfk, L0_attn_bfk, L0_ffn_norm_scale, L0_ffn_gate_w, L0_ffn_gate_b,
           L0_ffn_w1, L0_ffn_b1, L0_ffn_w2, L0_ffn_b2):
    import numpy as np
    import concourse.bacc as bacc
    from concourse.bass_utils import run_bass_kernel_spmd

    arr = {n: np.asarray(a) for n, a in (
        ("x", L0_attn_hidden_states), ("wq", L0_attn_Wq), ("bq", L0_attn_bq), ("wk", L0_attn_Wk), ("bk", L0_attn_bk),
        ("wv", L0_attn_Wv), ("bv", L0_attn_bv), ("wfq", L0_attn_Wfq), ("bfq", L0_attn_bfq), ("wfk", L0_attn_Wfk),
        ("bfk", L0_attn_bfk), ("nscale", L0_ffn_norm_scale), ("gw", L0_ffn_gate_w), ("gb", L0_ffn_gate_b),
        ("w1", L0_ffn_w1), ("b1", L0_ffn_b1), ("w2", L0_ffn_w2), ("b2", L0_ffn_b2))}
    w1 = arr["w1"].reshape(NE, H, 2, H)
    laid = [
        ("x", arr["x"].reshape(NTOK, H)),
        ("wq", arr["wq"]), ("bq", arr["bq"].reshape(H, 1)), ("wk", arr["wk"]), ("bk", arr["bk"].reshape(H, 1)),
        ("wvT", arr["wv"].T), ("bv", arr["bv"]), ("wfqT", arr["wfq"].T), ("bfq", arr["bfq"]),
        ("wfkT", arr["wfk"].T), ("bfk", arr["bfk"]),
        ("nscale", arr["nscale"].reshape(H, 1)), ("gwT", arr["gw"].T), ("gate_b", arr["gb"]),
        ("w12T", np.concatenate([w1.transpose(3, 0, 2, 1).reshape(H, NE, 2 * H), arr["w2"].transpose(2, 0, 1)],
                                axis=2).reshape(H, NE * EW)),
        ("b1", arr["b1"].reshape(NE, H, 2).transpose(0, 2, 1).reshape(NE, 2 * H)), ("b2", arr["b2"]),
    ]
    nc = bacc.Bacc("TRN2", target_bir_lowering=False, num_devices=1)
    arrays, args = {}, []
    for name, a in laid:
        a = np.ascontiguousarray(a)
        arrays["in_" + name] = a
        args.append(nc.dram_tensor("in_" + name, a.shape, mybir.dt.from_np(a.dtype), kind="ExternalInput").ap())
    out = nc.dram_tensor("out", (NTOK, H), F32, kind="ExternalOutput").ap()
    xs = [nc.dram_tensor(f"xs{c}", (SLOTS, H), F32, kind="Internal").ap() for c in range(NCHUNK)]
    ys = [nc.dram_tensor(f"ys{c}", (SLOTS, H), F32, kind="Internal").ap() for c in range(NCHUNK)]
    build(nc, *args, out, xs, ys)
    r = run_bass_kernel_spmd(nc, [arrays], core_ids=[0])
    return r.results[0]["out"].reshape(16, 256, H)
```

```python
from contextlib import ExitStack

import concourse.bass as bass
from concourse import mybir


P = 128
H = 128
NTOK = 4096
NTILE = NTOK // P
NCHUNK = 2
CT = NTILE // NCHUNK
NE = 32
TOPK = 4
PAIRS = CT * TOPK
GT = 4
EW = 3 * H
ST = -(-(CT * TOPK + NE - 1) // (2 * GT)) * 2 * GT
NG = ST // GT
GW = GT * H
SLOTS = ST * P
NB = CT // 2
NHEAD = 16
HD = H // NHEAD
EPS = 1e-5
LIMIT = 7.0
NPHASE = 2 * NCHUNK
NRG = CT // GT
CG = 4
NCG = CT // CG
KVW = H + NHEAD
NGF = NCHUNK * NG
COMB_A = NGF - CT
COMB_B = 2
CTB = CT * 5 // 8
STORE_LAG = 5

ALU = mybir.AluOpType
ACT = mybir.ActivationFunctionType
F32 = mybir.dt.float32
BF16 = mybir.dt.bfloat16
I32 = mybir.dt.int32
U32 = mybir.dt.uint32
X_AXIS = mybir.AxisListType.X


def sweep(eng, lead, n, tail, body, cut=None, late=None, steps=2):
    for k in range(lead):
        body(k, k % 2, k // 2)
    for first, stop, run in ((lead, cut or n, body), (cut or n, n, late)):
        if first < stop:
            assert (stop - first) % steps == 0 and first % 2 == 0
            with eng.Fori(0, (stop - first) // steps) as i:
                for j in range(steps):
                    run(i * steps + (first + j), j % 2, i * (steps // 2) + (first + j) // 2)
    for k in range(n, n + tail):
        (late or body)(k, k % 2, k // 2)


def live(k, lag, n):
    return not isinstance(k, int) or 0 <= k - lag < n


def wait_count(eng, sem, count):
    if not isinstance(count, int) or count > 0:
        eng.wait_ge(sem, count)


def build(nc, x, wq, bq, wk, bk, wvT, bv, wfqT, bfq, wfkT, bfk,
          nscale, gwT, gate_b, w12T, b1, b2, out, xs, ys):
    with ExitStack() as ctx:
        def sb(name, shape, dt=F32):
            return ctx.enter_context(nc.sbuf_tensor(name, shape, dt))

        def sem(name):
            return ctx.enter_context(nc.semaphore(name))

        X = sb("X", [P, NTILE * H])
        U = sb("U", [P, NTILE * H])
        W = sb("W", [P, NE * EW])
        YG = sb("YG", [P, PAIRS, H])
        xrow = sb("xrow", [P, 2, GW])
        xT = sb("xT", [P, 2, GW])
        glulin = sb("glulin", [P, 2, 2, GW])
        glu, lin = glulin[:, 0], glulin[:, 1]
        swish = sb("swish", [P, 2, GW])
        hid = sb("hid", [P, 2, GW])
        hidT = sb("hidT", [P, 2, GW])
        yrow = sb("yrow", [P, 2, GW])
        ident = sb("ident", [P, P])
        centre = sb("centre", [P, P])
        overH = sb("overH", [3, P], BF16)
        before = sb("before", [P, P], BF16)
        ones = sb("ones", [P, P], BF16)
        parts_on = sb("parts_on", [96, P], BF16)
        expert_no = sb("expert_no", [P, NE], BF16)
        slot_no = sb("slot_no", [NE, ST])
        steps128 = sb("steps128", [NE, CT])
        ends = sb("ends", [NE, NE], BF16)
        starts128 = sb("starts128", [NE, NE], BF16)
        headblock = sb("headblock", [P, H])
        headcol = sb("headcol", [P, NHEAD])
        scale_col = sb("scale_col", [P, 1])
        gw = sb("gw", [P, NE])
        gb_f = sb("gb_f", [96, NE])
        gb_r = sb("gb_r", [96, NE])
        gb_p = sb("gb_p", [96, NE], BF16)
        b1_f = sb("b1_f", [96, 2 * H])
        b1_r = sb("b1_r", [96, 2 * H])
        b1_p = sb("b1_p", [96, 2 * H], BF16)
        b1_3 = sb("b1_3", [3, NE * 2 * H], BF16)
        b2_s = sb("b2_s", [P, H])
        wq_s = sb("wq_s", [P, H])
        wk_s = sb("wk_s", [P, H])
        wfq_s = sb("wfq_s", [P, H])
        wfk_s = sb("wfk_s", [P, H])
        bqk_s = sb("bqk_s", [P, 2])
        qkvW = sb("qkvW", [P, 3 * H])
        abias_f = sb("abias_f", [96, 3 * H])
        abias_r = sb("abias_r", [96, 3 * H])
        abias_p = sb("abias_p", [96, 3 * H], BF16)
        st = sb("st", [P, NTILE * 6])
        sum2 = sb("sum2", [P, CT])
        dif = sb("dif", [P, CT])
        var = sb("var", [P, CT])
        vq = sb("vq", [P, 2 * CT])
        rs = sb("rs", [P, 2 * CT])
        nshift = sb("nshift", [P, CT])
        bscale = sb("bscale", [P, CT])
        bshift = sb("bshift", [P, CT])
        tT = xT
        top = sb("top", [P, CT * 8])
        topi = sb("topi", [P, CT * 8], U32)
        chosen = sb("chosen", [P, NCHUNK * PAIRS * NE], BF16)
        place = sb("place", [P, PAIRS * NE])
        mask = sb("mask", [P, CT * NE], BF16)
        counts = sb("counts", [NE, 1])
        over = sb("over", [NE, CT])
        ntiles = sb("ntiles", [NE, 1], BF16)
        span = sb("span", [NE, 1])
        ended = sb("ended", [NE, ST], BF16)
        eid = sb("eid", [1, NCHUNK * ST], I32)
        base = sb("base", [P, NE])
        where = sb("where", [P, CT * NE])
        pos = sb("pos", [P, PAIRS], I32)
        pos_a = sb("pos_a", [P, PAIRS], I32)
        pos_b = sb("pos_b", [P, PAIRS], I32)
        row = sb("row", [P, NCHUNK * PAIRS], I32)
        dlog = sb("dlog", [P, PAIRS])
        elog = sb("elog", [P, PAIRS])
        esum = sb("esum", [P, CT])
        erec = sb("erec", [P, CT])
        wtop = sb("wtop", [P, NCHUNK * PAIRS])
        arow = sb("arow", [P, 2, 2 * H])
        aT = hidT[:, 0].rearrange("p (s n) -> p s n", s=2)
        nmax = sb("nmax", [P, 2, 4])
        esm = swish[:].rearrange("p s (a h) -> p s a h", a=4)
        ssum = sb("ssum", [P, 2, 4])
        vext = sb("vext", [P, 2, 2, H + 2])
        qT = hidT[:, 1].rearrange("p (s n) -> p s n", s=2)
        kvd = sb("kvd", [P, 2, KVW])
        drec = sb("drec", [P, 2, NHEAD])
        ctxs = sb("ctxs", [P, 2, H])

        PS = ctx.enter_context(nc.psum_tensor("PS", [P, 8, 512], F32))
        TP = [PS[:, 0, :], PS[:, 1, :]]
        H1 = [PS[:, 2:4, :].rearrange("p a n -> p (a n)"), PS[:, 4:6, :].rearrange("p a n -> p (a n)")]
        HT = PS[:, 6, :]
        YP = PS[:, 7, :]
        LOG = [PS[:, 2, 0:GT * NE], PS[:, 5, 0:GT * NE]]
        RANK = PS[:, 3, :]
        CNT = PS[0:NE, 4, 0:1]
        SPAN = PS[0:NE, 4, 2:3]
        BASE = PS[:, 4, 4:4 + NE]
        EID = PS[0:1, 4, 64:64 + ST]
        KV = PS[:, 6, 0:H + 2]
        CTX = PS[:, 7, 0:2 * KVW].rearrange("p (a n) -> p a n", a=2)

        x_loaded = [sem(f"x_loaded{g}") for g in range(NRG)]
        x_rest_loaded = sem("x_rest_loaded")
        router_loaded = sem("router_loaded")
        b_loaded = sem("b_loaded")
        attn_loaded = sem("attn_loaded")
        w_loaded = sem("w_loaded")
        zero_ready = sem("zero_ready")
        filled = [sem(f"filled{c}") for c in range(NCHUNK)]
        const_step = sem("const_step")
        chain = sem("chain")
        stats_done = [sem(f"stats_done{c}") for c in range(NCHUNK)]
        var_ready = sem("var_ready")
        std_ready = sem("std_ready")
        norm_ready = sem("norm_ready")
        u_done = sem("u_done")
        u2_done = sem("u2_done")
        res_ready = sem("res_ready")
        base_done = sem("base_done")
        weighted = sem("weighted")
        b2_turned = sem("b2_turned")
        b2_copied = sem("b2_copied")
        b2_done = sem("b2_done")
        b2_added = sem("b2_added")
        uT_done = sem("uT_done")
        tT_done = sem("tT_done")
        logits_done = sem("logits_done")
        top_done = sem("top_done")
        topi_done = sem("topi_done")
        dlog_ready = sem("dlog_ready")
        elog_ready = sem("elog_ready")
        mask_ready = sem("mask_ready")
        counted = sem("counted")
        ntiles_ready = sem("ntiles_ready")
        spans_done = sem("spans_done")
        ended_ready = sem("ended_ready")
        eid_done = sem("eid_done")
        rows_ready = sem("rows_ready")
        route_done = sem("route_done")
        scattered = [sem(f"scattered{c}") for c in range(NCHUNK)]
        xrow_loaded = [sem(f"xrow_loaded{r}") for r in range(2)]
        x_turned = sem("x_turned")
        xT_ready = sem("xT_ready")
        h1_done = sem("h1_done")
        glu_ready = sem("glu_ready")
        lin_ready = sem("lin_ready")
        swish_ready = sem("swish_ready")
        hid_ready = sem("hid_ready")
        hid_turned = sem("hid_turned")
        hidT_ready = sem("hidT_ready")
        y_done = sem("y_done")
        yrow_ready = sem("yrow_ready")
        yrow_stored = [sem(f"yrow_stored{r}") for r in range(2)]
        gathered = [sem(f"gathered{r}") for r in range(2)]
        combined = sem("combined")
        fold_done = sem("fold_done")
        fold_copied = sem("fold_copied")
        bias_ready = sem("bias_ready")
        centre_ready = sem("centre_ready")
        shift_done = sem("shift_done")
        w_ready = sem("w_ready")
        b1_spread = sem("b1_spread")
        arow_ready = sem("arow_ready")
        a_turned = sem("a_turned")
        aT_ready = sem("aT_ready")
        qkv_done = sem("qkv_done")
        nmax_ready = sem("nmax_ready")
        esm_ready = sem("esm_ready")
        v_copied = sem("v_copied")
        q_turned = sem("q_turned")
        qT_ready = sem("qT_ready")
        kv_done = sem("kv_done")
        kvd_ready = sem("kvd_ready")
        ctx_done = sem("ctx_done")
        drec_ready = sem("drec_ready")
        ctxs_ready = sem("ctxs_ready")
        srec_ready = sem("srec_ready")
        attn_done = sem("attn_done")
        based = sem("based")
        out_stored = sem("out_stored")

        x_v = x.rearrange("(c t p) h -> c p t h", c=NCHUNK, p=P)
        out_v = out.rearrange("(g t p) h -> g p t h", t=CG, p=P)
        xs_v = [a.rearrange("(g p q) h -> g p (q h)", p=P, q=GT) for a in xs]
        ys_v = [a.rearrange("(g p q) h -> g p (q h)", p=P, q=GT) for a in ys]
        zero = YG[:, 0:PAIRS // 2, :].rearrange("p a h -> p (a h)")
        ZW = PAIRS // 2 * H
        NZ = SLOTS * H // (P * ZW)
        assert NZ * P * ZW == SLOTS * H

        NROUTER, NB12, NATTN, NW = 3, 3 + TOPK, 7 + 3, 1
        NCONST = 20

        def w1_pair(k):
            return W[:, bass.ds(k * (2 * EW), 2 * EW)].rearrange("p (e n) -> p e n", n=EW)[:, :, 0:2 * H]

        block = ctx.enter_context(nc.Block())

        @block.sync
        def _(sp):
            for g in range(NRG):
                t = slice(g * GT, (g + 1) * GT)
                sp.dma_start(X[:, g * GW:(g + 1) * GW].rearrange("p (t h) -> p t h", h=H), x_v[0][:, t])\
                    .then_inc(x_loaded[g], 16)
            sp.dma_start(scale_col[:], nscale).then_inc(router_loaded, 16)
            sp.dma_start(gw[:], gwT).then_inc(router_loaded, 16)
            sp.dma_start(gb_f[:], gate_b.partition_broadcast(96)).then_inc(router_loaded, 16)
            for r in range(3):
                sp.dma_start(b1_f[NE * r:NE * r + NE, :], b1).then_inc(b_loaded, 16)
            for k in range(TOPK):
                sp.dma_start(b2_s[NE * k:NE * k + NE, :], b2).then_inc(b_loaded, 16)
            sp.wait_ge(zero_ready, 1)
            for c in range(NCHUNK):
                for z in range(NZ):
                    sp.dma_start(xs[c].rearrange("(z p a) h -> z p (a h)", z=NZ, p=P)[z], zero)\
                        .then_inc(filled[c], 16)
                if c == 0:
                    for d in range(1, NCHUNK):
                        sp.dma_start(X[:, d * CT * H:(d + 1) * CT * H].rearrange("p (t h) -> p t h", h=H),
                                     x_v[d]).then_inc(x_rest_loaded, 16)
                    sp.dma_start(W[:], w12T).then_inc(w_loaded, 16)
                    for dst, src in ((wq_s, wq), (wk_s, wk), (wfq_s, wfqT), (wfk_s, wfkT)):
                        sp.dma_start(dst[:], src).then_inc(attn_loaded, 16)
                    sp.dma_start(qkvW[:, 2 * H:3 * H], wvT).then_inc(attn_loaded, 16)
                    sp.dma_start(bqk_s[:, 0:1], bq).then_inc(attn_loaded, 16)
                    sp.dma_start(bqk_s[:, 1:2], bk).then_inc(attn_loaded, 16)
                    for n, src in enumerate((bfq, bfk, bv)):
                        sp.dma_start(abias_f[:, n * H:(n + 1) * H], src.partition_broadcast(96)).then_inc(attn_loaded, 16)

            sp.wait_ge(bias_ready, 2)
            for q in range(3):
                sp.dma_start(b1_3[q:q + 1, :].rearrange("o (e n) -> o e n", n=2 * H), b1_p[NE * q:NE * q + NE, :])\
                    .then_inc(b1_spread, 16)

            def experts(f):
                def load(c, k, r):
                    wait_count(sp, x_turned, k + (f * NGF + c * NG - 1))
                    sp.dma_start(xrow[:, r, :], xs_v[c][bass.ds(k, 1)].rearrange("g p n -> (g p) n"))\
                        .then_inc(xrow_loaded[r], 16)

                def store(c, k, r):
                    sp.wait_ge(yrow_ready, k + (f * NGF + c * NG + 1))
                    sp.dma_start(ys_v[c][bass.ds(k, 1)].rearrange("g p n -> (g p) n"), yrow[:, r, :])\
                        .then_inc(yrow_stored[r], 16)

                lead = STORE_LAG + 1
                for c in range(NCHUNK):
                    sp.wait_ge(scattered[c], 16 * PAIRS * (f + 1))
                    for k in range(lead):
                        load(c, k, k % 2)
                        if k >= STORE_LAG:
                            store(c, k - STORE_LAG, (k - STORE_LAG) % 2)
                        elif c:
                            store(c - 1, NG + k - STORE_LAG, (k - STORE_LAG) % 2)
                    with sp.Fori(0, (NG - lead) // 2) as i:
                        for r in range(2):
                            load(c, i * 2 + (lead + r), r)
                            store(c, i * 2 + (lead + r - STORE_LAG), (r + STORE_LAG) % 2)
                for k in range(NG - STORE_LAG, NG):
                    store(NCHUNK - 1, k, k % 2)

            for f in range(2):
                experts(f)
            for c in range(NCHUNK):
                for g in range(NCG):
                    sp.wait_ge(b2_added, NCHUNK * NRG + c * NRG + (g + 1) * CG // GT)
                    sp.wait_ge(combined, PAIRS * (NCHUNK + c) + CG * TOPK * (g + 1))
                    t = c * CT + g * CG
                    sp.dma_start(out_v[c * NCG + g], X[:, t * H:(t + CG) * H].rearrange("p (t h) -> p t h", h=H))\
                        .then_inc(out_stored, 16)
            sp.wait_ge(out_stored, 16 * NCHUNK * NCG)

        @block.gpsimd
        def _(pool):
            made = [0]

            def step(ins):
                made[0] += 1
                ins.then_inc(const_step, 1)

            g = nc.gpsimd
            step(g.memset(ident[:], 0.0))
            step(g.memset(before[:], 1.0))
            step(g.memset(centre[:], -1.0 / H))
            step(g.memset(overH[:], 1.0 / H))
            step(g.memset(ends[:], 1.0))
            step(g.memset(starts128[:], 128.0))
            step(g.memset(headblock[:], 1.0))
            step(g.memset(headcol[:], 1.0))
            step(g.memset(ones[:], 1.0))
            step(g.iota(expert_no[:], [[1, NE]], base=0, channel_multiplier=0, allow_small_or_imprecise_dtypes=True))
            step(g.iota(slot_no[:], [[1, ST]], base=0, channel_multiplier=0, allow_small_or_imprecise_dtypes=True))
            step(g.iota(steps128[:], [[P, CT]], base=0, channel_multiplier=0, allow_small_or_imprecise_dtypes=True))
            pool.wait_ge(const_step, made[0])
            step(g.affine_select(out=ident[:], in_=ident[:], compare_op=ALU.not_equal, fill=1.0, base=0,
                                 pattern=[[-1, P]], channel_multiplier=1))
            step(g.affine_select(out=before[:], in_=before[:], compare_op=ALU.is_ge, fill=0.0, base=-1,
                                 pattern=[[1, P]], channel_multiplier=-1))
            step(g.affine_select(out=ends[:], in_=ends[:], compare_op=ALU.is_ge, fill=0.0,
                                 base=0, pattern=[[1, NE]], channel_multiplier=-1))
            step(g.affine_select(out=starts128[:], in_=starts128[:], compare_op=ALU.is_ge, fill=0.0,
                                 base=-1, pattern=[[1, NE]], channel_multiplier=-1))
            hb = headblock[:].rearrange("p (b d) -> p b d", d=HD)
            step(g.affine_select(out=hb, in_=hb, compare_op=ALU.is_ge, fill=0.0,
                                 base=0, pattern=[[-HD, NHEAD], [0, HD]], channel_multiplier=1))
            step(g.affine_select(out=headcol[:], in_=headcol[:], compare_op=ALU.is_ge, fill=0.0,
                                 base=0, pattern=[[-HD, NHEAD]], channel_multiplier=1))
            pool.wait_ge(const_step, made[0])
            step(g.affine_select(out=hb, in_=hb, compare_op=ALU.is_ge, fill=0.0,
                                 base=HD - 1, pattern=[[HD, NHEAD], [0, HD]], channel_multiplier=-1))
            step(g.affine_select(out=headcol[:], in_=headcol[:], compare_op=ALU.is_ge, fill=0.0,
                                 base=HD - 1, pattern=[[HD, NHEAD]], channel_multiplier=-1))
            assert made[0] == NCONST
            g.memset(YG[:, 0:PAIRS // 2, :], 0.0).then_inc(zero_ready, 1)

            def scatter(ph):
                c = ph % NCHUNK
                pool.wait_ge(u_done, CT // 2 * (ph + 1))
                pool.wait_ge(u2_done, CT // 2 * (ph + 1))
                pool.wait_ge(rows_ready, CT * ph + GT)
                if ph < NCHUNK:
                    pool.wait_ge(filled[c], 16 * NZ)
                for t in range(CT):
                    if t and t % GT == 0:
                        pool.wait_ge(rows_ready, CT * ph + t + GT)
                    for k in range(TOPK):
                        i = c * PAIRS + t * TOPK + k
                        pool.indirect_dma_start(
                            out=xs[c], out_offset=bass.IndirectOffsetOnAxis(ap=row[:, i:i + 1], axis=0),
                            in_=U[:, (c * CT + t) * H:(c * CT + t + 1) * H], in_offset=None,
                        ).then_inc(scattered[c], 16)

            def gather(ph):
                c = ph % NCHUNK
                for r in range(2):
                    pool.wait_ge(yrow_stored[r], 16 * (NG // 2) * (ph + 1))
                if ph == 0:
                    for d in range(NCHUNK):
                        pool.wait_ge(filled[d], 16 * NZ)
                for t in range(CT):
                    if ph and t % CG == 0:
                        pool.wait_ge(combined, PAIRS * (ph - 1) + TOPK * (t + CG))
                    wait_count(pool, gathered[t % 2], 16 * TOPK * ((ph * CT + t) // 2))
                    for k in range(TOPK):
                        i = c * PAIRS + t * TOPK + k
                        pool.indirect_dma_start(
                            out=YG[:, t * TOPK + k, :], out_offset=None,
                            in_=ys[c], in_offset=bass.IndirectOffsetOnAxis(ap=row[:, i:i + 1], axis=0),
                        ).then_inc(gathered[t % 2], 16)

            for f in range(2):
                for c in range(NCHUNK):
                    scatter(f * NCHUNK + c)
                for c in range(NCHUNK):
                    gather(f * NCHUNK + c)

        @block.scalar
        def _(act):
            a = nc.scalar

            def normalise(n):
                act.wait_ge(var_ready, n + 1)
                a.activation(vq[:], vq[:], ACT.Sqrt).then_inc(std_ready, 1)

            def route(ph, n):
                c = ph % NCHUNK
                normalise(n)
                act.wait_ge(norm_ready, n + 1)
                if ph >= NCHUNK:
                    act.wait_ge(scattered[c], 16 * PAIRS * (ph // NCHUNK))

                def rows(first, stop):
                    for t in range(first, stop):
                        i = (c * CT + t) * H
                        a.activation(U[:, i:i + H], X[:, i:i + H], ACT.Identity, scale=rs[:, CT + t:CT + t + 1],
                                     bias=nshift[:, t:t + 1]).then_inc(u_done, 1)

                rows(0, GT + 2)
                if ph == 0:
                    act.wait_ge(router_loaded, 16 * NROUTER)
                for q in range(NRG):
                    Q = ph * NRG + q
                    act.wait_ge(uT_done, Q + 1)
                    wait_count(act, logits_done, Q - 1)
                    a.activation(tT[:, q % 2, :], TP[q % 2], ACT.Copy, scale=scale_col[:, 0:1]).then_inc(tT_done, 1)
                    if q == 0:
                        rows(GT + 2, CT // 2)
                act.wait_ge(res_ready, ph + 1)
                for t in range(CT):
                    xt = X[:, (c * CT + t) * H:(c * CT + t + 1) * H]
                    if t < CT // 2:
                        act.wait_ge(u_done, CT // 2 * ph + t + 1)
                    else:
                        act.wait_ge(u2_done, CT // 2 * (ph - 1) + t + 1)
                    a.activation(xt, xt, ACT.Identity, scale=bscale[:, t:t + 1], bias=bshift[:, t:t + 1])\
                        .then_inc(base_done, 1)
                act.wait_ge(dlog_ready, ph + 1)
                a.activation(elog[:], dlog[:], ACT.Exp).then_inc(elog_ready, 1)

            def experts(f):
                g0 = f * NGF

                def step(k, r, m):
                    s = 1 - r
                    if live(k, 0, NGF):
                        act.wait_ge(x_turned, k + (g0 + 1))
                        wait_count(act, h1_done, k + (g0 - 1))
                        a.activation(xT[:, r, :], TP[r], ACT.Copy, bias=1.0).then_inc(xT_ready, 1)
                    if live(k, 4, NGF):
                        act.wait_ge(y_done, k + (g0 - 3))
                        wait_count(act, yrow_stored[r], (m + (g0 // 2 - 2)) * 16)
                        a.activation(yrow[:, r, :], YP, ACT.Copy).then_inc(yrow_ready, 1)
                    if live(k, 3, NGF):
                        act.wait_ge(hid_turned, k + (g0 - 2))
                        wait_count(act, y_done, k + (g0 - 4))
                        a.activation(hidT[:, s, :], HT, ACT.Copy).then_inc(hidT_ready, 1)
                    if live(k, 1, NGF):
                        act.wait_ge(glu_ready, k + g0)
                        wait_count(act, hid_ready, k + (g0 - 2))
                        a.activation(swish[:, s, :], glu[:, s, :], ACT.Gelu_apprx_sigmoid).then_inc(swish_ready, 1)

                sweep(act, 8, NGF, 4, step, steps=4)

            def attention(c, n):
                n0 = c * NB
                normalise(n)
                act.wait_ge(norm_ready, n + 1)

                def norm_rows(k, s):
                    wait_count(act, a_turned, k + (n0 - 1))
                    for i in range(2):
                        t = k * 2 + i
                        a.activation(arow[:, s, i * H:(i + 1) * H], X[:, bass.ds((t + c * CT) * H, H)], ACT.Identity,
                                     scale=rs[:, bass.ds(t, 1)], bias=nshift[:, bass.ds(t, 1)]).then_inc(arow_ready, 1)

                def step(k, r, m):
                    s = 1 - r
                    if live(k, -1, NB):
                        norm_rows(k + 1, s)
                    if live(k, 0, NB):
                        act.wait_ge(a_turned, k + (n0 + 1))
                        wait_count(act, qkv_done, k + (n0 - 1))
                        a.activation(aT[:, r, :], PS[:, 0, 0:2 * H], ACT.Copy).then_inc(aT_ready, 1)
                    if live(k, 2, NB):
                        act.wait_ge(q_turned, k + (n0 - 1))
                        wait_count(act, ctx_done, k + (n0 - 3))
                        a.activation(qT[:, r, :], PS[:, 1, 0:2 * H], ACT.Copy).then_inc(qT_ready, 1)
                    if live(k, 1, NB):
                        act.wait_ge(nmax_ready, k + n0)
                        wait_count(act, kv_done, k + (n0 - 2))
                        for i in range(4):
                            a.activation(esm[:, s, i, :], PS[:, 2 + 2 * s + i // 2, (i % 2) * H:(i % 2 + 1) * H], ACT.Exp,
                                         bias=nmax[:, s, i:i + 1], accum_out=ssum[:, s, i:i + 1]).then_inc(esm_ready, 1)
                    if c == 0 and live(k, 1, NB):
                        act.wait_ge(srec_ready, k + n0)
                        for i in range(2):
                            a.activation(vext[:, s, i, 0:H], PS[:, 2 + 2 * s + i, 2 * H:3 * H], ACT.Copy,
                                         scale=vext[:, s, i, H:H + 1]).then_inc(v_copied, 1)

                norm_rows(0, 0)
                sweep(act, 4, NB - 2, 5, step)

            for c in range(NCHUNK):
                route(c, c)

            def shifted_w1(k, r, m):
                act.wait_ge(shift_done, k + 1)
                a.activation(w1_pair(k), PS[:, 2 + r, :].rearrange("p (e n) -> p e n", e=2), ACT.Copy).then_inc(w_ready, 1)

            sweep(act, 0, NE // 2, 0, shifted_w1)

            def add_b2(f):
                for n in range(f * NCHUNK * NRG, (f + 1) * NCHUNK * NRG):
                    act.wait_ge(b2_turned, n + 1)
                    wait_count(act, b2_done, n - 1)
                    a.activation(xT[:, n % 2, :], TP[n % 2], ACT.Copy).then_inc(b2_copied, 1)

            add_b2(0)
            experts(0)
            for c in range(NCHUNK):
                attention(c, NCHUNK + 2 * c)
                route(NCHUNK + c, NCHUNK + 2 * c + 1)
            experts(1)
            add_b2(1)

        @block.vector
        def _(dve):
            v = nc.vector
            linked = [0]

            def link(ins):
                linked[0] += 1
                ins.then_inc(chain, 1)
                dve.wait_ge(chain, linked[0])

            def stats(t, c):
                v.bn_stats(st[:, bass.ds(t * 6, 6)], X[:, bass.ds(t * H, H)]).then_inc(stats_done[c], 1)

            def normalise(c, done, n, rows):
                dve.wait_ge(stats_done[c], CT * done)
                s6 = st[:, c * CT * 6:(c + 1) * CT * 6].rearrange("p (t s) -> p s t", s=6)
                linked[0] += 2
                v.tensor_tensor(sum2[:], s6[:, 1, :], s6[:, 4, :], ALU.add).then_inc(chain, 1)
                v.tensor_tensor(dif[:], s6[:, 1, :], s6[:, 4, :], ALU.subtract).then_inc(chain, 1)
                link(v.tensor_tensor(var[:], s6[:, 2, :], s6[:, 5, :], ALU.add))
                link(v.scalar_tensor_tensor(dif[:], dif[:], 0.25, dif[:], ALU.mult, ALU.mult))
                link(v.scalar_tensor_tensor(var[:], var[:], 1.0 / H, dif[:], ALU.mult, ALU.add))
                link(v.tensor_scalar(vq[:, 0:CT], var[:], EPS, None, ALU.add))
                v.scalar_tensor_tensor(vq[:, CT:2 * CT], vq[:, 0:CT], EPS, var[:], ALU.mult, ALU.add)\
                    .then_inc(var_ready, 1)
                dve.wait_ge(std_ready, n + 1)
                link(v.reciprocal(rs[:], vq[:]))
                v.scalar_tensor_tensor(nshift[:], sum2[:], -0.5, rs[:, rows], ALU.mult, ALU.mult)\
                    .then_inc(norm_ready, 1)

            def route(ph, n, between=None):
                c = ph % NCHUNK
                normalise(c, 1 if ph < NCHUNK else 3, n, slice(CT, 2 * CT))
                link(v.tensor_scalar(bscale[:], rs[:, 0:CT], 0.5, 1.0, ALU.mult, ALU.add))
                v.scalar_tensor_tensor(bshift[:], sum2[:], -0.25, rs[:, 0:CT], ALU.mult, ALU.mult).then_inc(res_ready, 1)
                dve.wait_ge(norm_ready, n + 1)
                if ph >= NCHUNK:
                    dve.wait_ge(scattered[c], 16 * PAIRS * (ph // NCHUNK))
                for t in range(CT // 2, CT):
                    i = (c * CT + t) * H
                    v.tensor_scalar(U[:, i:i + H], X[:, i:i + H], rs[:, CT + t:CT + t + 1], nshift[:, t:t + 1],
                                    ALU.mult, ALU.add).then_inc(u2_done, 1)
                if between:
                    between()
                if ph == 0:
                    dve.wait_ge(router_loaded, 16 * NROUTER)
                    split(gb_f, gb_r, gb_p)
                    dve.wait_ge(const_step, NCONST)
                for q in range(NRG):
                    Q = ph * NRG + q
                    tiles = range(q * GT, (q + 1) * GT)
                    dve.wait_ge(logits_done, Q + 1)
                    for t in tiles:
                        lg = LOG[q % 2][:, (t - q * GT) * NE:(t - q * GT + 1) * NE]
                        v.max(top[:, t * 8:t * 8 + 8], lg).then_inc(top_done, 1)
                    for t in tiles:
                        dve.wait_ge(top_done, CT * ph + t + 1)
                        lg = LOG[q % 2][:, (t - q * GT) * NE:(t - q * GT + 1) * NE]
                        v.max_index(topi[:, t * 8:t * 8 + 8], top[:, t * 8:t * 8 + 8], lg)\
                            .then_inc(topi_done, 1)
                    dve.wait_ge(topi_done, CT * ph + (q + 1) * GT)
                    ti = topi[:, q * GT * 8:(q + 1) * GT * 8].rearrange("p (t k o) -> p t k o", k=8, o=1)[:, :, 0:TOPK]
                    ch = chosen[:, (c * CT + q * GT) * TOPK * NE:(c * CT + (q + 1) * GT) * TOPK * NE]
                    link(v.tensor_tensor(ch.rearrange("p (t k e) -> p t k e", k=TOPK, e=NE),
                                         expert_no[:].rearrange("p (a o e) -> p a o e", a=1, o=1)
                                         .broadcast_to([P, GT, TOPK, NE]),
                                         ti.broadcast_to([P, GT, TOPK, NE]), ALU.is_equal))
                    with nc.allow_low_precision(reason="sums of at most one 1"):
                        v.tensor_reduce(mask[:, q * GT * NE:(q + 1) * GT * NE].rearrange("p (t e) -> p t e", e=NE),
                                        ch.rearrange("p (t k e) -> p t e k", k=TOPK, e=NE), X_AXIS, ALU.add)\
                            .then_inc(mask_ready, 1)
                t8 = top[:].rearrange("p (t k) -> p t k", k=8)
                tk = [P, CT, TOPK]
                v.tensor_tensor(dlog[:].rearrange("p (t k) -> p t k", k=TOPK), t8[:, :, 0:TOPK],
                                t8[:, :, 0:1].broadcast_to(tk), ALU.subtract).then_inc(dlog_ready, 1)
                dve.wait_ge(counted, ph + 1)
                link(v.tensor_copy(counts[:], CNT))
                link(v.tensor_scalar(over[:], steps128[:], counts[:, 0:1], None, ALU.is_lt))
                with nc.allow_low_precision(reason="integers up to 16"):
                    v.tensor_reduce(ntiles[:], over[:], X_AXIS, ALU.add).then_inc(ntiles_ready, 1)
                dve.wait_ge(spans_done, ph + 1)
                v.tensor_copy(base[:], BASE).then_inc(based, 1)
                v.tensor_copy(span[:], SPAN).then_inc(based, 1)
                dve.wait_ge(based, 2 * ph + 2)

                def begins(first, stop):
                    link(v.tensor_tensor(where[:, first * NE:stop * NE].rearrange("p (t e) -> p t e", e=NE),
                                         RANK[:, first * NE:stop * NE].rearrange("p (t e) -> p t e", e=NE),
                                         base[:].rearrange("p (o e) -> p o e", o=1)
                                         .broadcast_to([P, stop - first, NE]), ALU.add))

                def slots(first, stop):
                    n = stop - first
                    pr = slice(first * TOPK, stop * TOPK)
                    ch = chosen[:, (c * CT + first) * TOPK * NE:(c * CT + stop) * TOPK * NE]
                    pl = place[:, first * TOPK * NE:stop * TOPK * NE]
                    link(v.tensor_tensor(pl.rearrange("p (t k e) -> p t k e", k=TOPK, e=NE),
                                         ch.rearrange("p (t k e) -> p t k e", k=TOPK, e=NE),
                                         where[:, first * NE:stop * NE].rearrange("p (t o e) -> p t o e", o=1, e=NE)
                                         .broadcast_to([P, n, TOPK, NE]), ALU.mult))
                    with nc.allow_low_precision(reason="one integer and zeros"):
                        link(v.tensor_reduce(pos[:, pr], pl.rearrange("p (t e) -> p t e", e=NE), X_AXIS, ALU.add))

                def slots_to_rows(first, stop):
                    pr = slice(first * TOPK, stop * TOPK)
                    link(v.tensor_scalar(pos_a[:, pr], pos[:, pr], P - 1, 2, ALU.bitwise_and, ALU.logical_shift_left))
                    link(v.tensor_scalar(pos_b[:, pr], pos[:, pr], 7, GT - 1, ALU.logical_shift_right, ALU.bitwise_and))
                    link(v.tensor_tensor(pos_a[:, pr], pos_a[:, pr], pos_b[:, pr], ALU.bitwise_or))
                    link(v.tensor_scalar(pos_b[:, pr], pos[:, pr], 9, 9, ALU.logical_shift_right, ALU.logical_shift_left))
                    v.tensor_tensor(row[:, c * PAIRS + first * TOPK:c * PAIRS + stop * TOPK], pos_a[:, pr], pos_b[:, pr],
                                    ALU.bitwise_or).then_inc(rows_ready, stop - first)

                def tile_experts():
                    dve.wait_ge(eid_done, ph + 1)
                    v.tensor_scalar(eid[:, c * ST:(c + 1) * ST], EID, float(NE - 1), float(EW), ALU.min, ALU.mult)\
                        .then_inc(route_done, 1)

                def end():
                    v.tensor_scalar(ended[:], slot_no[:], span[:, 0:1], None, ALU.is_ge).then_inc(ended_ready, 1)

                def rows(first, stop):
                    slots(first, stop)
                    slots_to_rows(first, stop)

                if c == NCHUNK - 1:
                    end()
                    begins(0, CT)
                    tile_experts()
                    rows(0, GT)
                else:
                    begins(0, GT)
                    rows(0, GT)
                    end()
                    begins(GT, CT)
                    tile_experts()

                def weights():
                    dve.wait_ge(elog_ready, ph + 1)
                    el = elog[:].rearrange("p (t k) -> p t k", k=TOPK)
                    link(v.tensor_reduce(esum[:], el, X_AXIS, ALU.add))
                    link(v.reciprocal(erec[:], esum[:]))
                    link(v.scalar_tensor_tensor(wtop[:, c * PAIRS:(c + 1) * PAIRS].rearrange("p (t k) -> p t k", k=TOPK),
                                                el, 0.5, erec[:].rearrange("p (t o) -> p t o", o=1).broadcast_to(tk),
                                                ALU.mult, ALU.mult))

                return slots, slots_to_rows, weights

            def split(src, rest, dst):
                link(v.tensor_copy(dst[:], src[:]))
                link(v.tensor_tensor(rest[:], src[:], dst[:], ALU.subtract))
                for q in (1, 2):
                    link(v.tensor_copy(dst[NE * q:NE * q + NE, :], rest[NE * q:NE * q + NE, :]))
                link(v.tensor_tensor(rest[64:96, :], rest[64:96, :], dst[64:96, :], ALU.subtract))
                v.tensor_copy(dst[64:96, :], rest[64:96, :]).then_inc(bias_ready, 1)

            class Combine:

                def __init__(self, t, r, m, c, f):
                    self.t, self.r, self.m, self.c, self.f, self.ph = t, r, m, c, f, f * NCHUNK + c

                def add(self, j):
                    t, base = self.t, PAIRS * self.ph
                    if j == 0:
                        dve.wait_ge(gathered[self.r], (self.m + (self.ph * CT // 2 + 1)) * (16 * TOPK))
                    else:
                        dve.wait_ge(combined, t * TOPK + (base + j))
                    xt = X[:, bass.ds(t * H + self.c * CT * H, H)]
                    v.scalar_tensor_tensor(xt, YG[:, bass.ds(t * TOPK + j, 1), :].rearrange("p o h -> p (o h)"),
                                           wtop[:, bass.ds(t * TOPK + (self.c * PAIRS + j), 1)], xt,
                                           ALU.mult, ALU.add).then_inc(combined, 1)

                def stats(self):
                    dve.wait_ge(combined, self.t * TOPK + (PAIRS * self.ph + TOPK))
                    stats(self.t + self.c * CT, self.c)

            def experts(f, beside=()):
                g0 = f * NGF

                def step(k, r, m, combining=False):
                    s = 1 - r
                    h1 = H1[s].rearrange("p (q g f) -> p g q f", q=GT, g=2)
                    adding = combining and live(k, COMB_A, CT)
                    tile = Combine(k - COMB_A, r, m - COMB_A // 2, 0, f)

                    def add(j):
                        if adding:
                            tile.add(j)

                    add(0)
                    if live(k, 1, NGF):
                        dve.wait_ge(h1_done, k + g0)
                        wait_count(dve, swish_ready, k + (g0 - 2))
                        v.tensor_scalar(glu[:, s, :].rearrange("p (q f) -> p q f", q=GT), h1[:, 0],
                                        LIMIT, None, ALU.min).then_inc(glu_ready, 1)
                    add(1)
                    if live(k, 1, NGF):
                        wait_count(dve, hid_ready, k + (g0 - 2))
                        v.tensor_scalar(lin[:, s, :].rearrange("p (q f) -> p q f", q=GT), h1[:, 1],
                                        -LIMIT, LIMIT, ALU.max, ALU.min).then_inc(lin_ready, 1)
                    add(2)
                    if live(k, 1, NGF):
                        dve.wait_ge(swish_ready, k + g0)
                        dve.wait_ge(lin_ready, k + g0)
                        wait_count(dve, hid_turned, k + (g0 - 2))
                        v.scalar_tensor_tensor(hid[:, s, :], lin[:, s, :], 1.0, swish[:, s, :], ALU.add, ALU.mult)\
                            .then_inc(hid_ready, 1)
                    add(3)
                    if isinstance(k, int) and 1 <= k <= len(beside):
                        beside[k - 1]()
                    if adding and f == 0:
                        tile.stats()

                if f == 0:
                    dve.wait_ge(b2_added, NCHUNK * NRG)
                dve.wait_ge(base_done, CT * (f * NCHUNK + 1))
                sweep(dve, 8, NGF, 2, step, COMB_A, lambda k, r, m: step(k, r, m, True), steps=4)

            def combine(ph, first, stop):
                c = ph % NCHUNK
                dve.wait_ge(b2_added, (ph + 1) * NRG)
                for t0 in range(first, stop, 2):
                    for r in range(2):
                        dve.wait_ge(gathered[r], 16 * TOPK * ((ph * CT + t0) // 2 + 1))
                    for k in range(TOPK):
                        for t in (t0, t0 + 1):
                            if k:
                                dve.wait_ge(combined, PAIRS * ph + TOPK * t0 + 2 * (k - 1) + t % 2 + 1)
                            xt = X[:, (c * CT + t) * H:(c * CT + t + 1) * H]
                            w = c * PAIRS + t * TOPK + k
                            v.scalar_tensor_tensor(xt, YG[:, t * TOPK + k, :], wtop[:, w:w + 1], xt,
                                                   ALU.mult, ALU.add).then_inc(combined, 1)
                    if ph < NCHUNK:
                        for t in (t0, t0 + 1):
                            dve.wait_ge(combined, PAIRS * ph + TOPK * (t0 + 2) - 2 + t % 2 + 1)
                            stats(c * CT + t, c)

            def attention(c, n, beside=None):
                n0 = c * NB
                normalise(c, 2, n, slice(0, CT))
                if beside:
                    beside()

                def step(k, r, m):
                    s = 1 - r
                    tile = Combine(k - COMB_B, r, m - COMB_B // 2, NCHUNK - 1, 0) if c == 0 else None

                    def add(j):
                        if tile and live(k, COMB_B, CTB):
                            tile.add(j)

                    if live(k, 1, NB):
                        dve.wait_ge(qkv_done, k + n0)
                        v.tensor_reduce(nmax[:, s, :].rearrange("p (a b) -> p a b", a=2),
                                        PS[:, 2 + 2 * s:4 + 2 * s, 0:2 * H].rearrange("p a (b h) -> p a b h", b=2),
                                        X_AXIS, ALU.max, negate=True).then_inc(nmax_ready, 1)
                    add(0)
                    if live(k, 3, NB):
                        dve.wait_ge(ctx_done, k + (n0 - 2))
                        v.reciprocal(drec[:], CTX[:, :, H:KVW]).then_inc(drec_ready, 1)
                        add(1)
                        dve.wait_ge(drec_ready, k + (n0 - 2))
                        v.tensor_tensor(ctxs[:].rearrange("p a (h d) -> p a h d", d=HD),
                                        CTX[:, :, 0:H].rearrange("p a (h d) -> p a h d", d=HD),
                                        drec[:].rearrange("p a (h o) -> p a h o", o=1).broadcast_to([P, 2, NHEAD, HD]),
                                        ALU.mult).then_inc(ctxs_ready, 1)
                        add(2)
                        dve.wait_ge(ctxs_ready, k + (n0 - 2))
                        xt = X[:, bass.ds((k - 3) * (2 * H) + c * CT * H, 2 * H)]
                        v.tensor_tensor(xt, xt, ctxs[:].rearrange("p a n -> p (a n)"), ALU.add).then_inc(attn_done, 1)
                    else:
                        add(1)
                        add(2)
                    if live(k, 1, NB):
                        dve.wait_ge(esm_ready, (k + n0) * 4)
                        wait_count(dve, kv_done, k + (n0 - 2))
                        v.reciprocal(vext[:, s, :, H:H + 1],
                                     ssum[:, s, :].rearrange("p (a b) -> p a b", b=2)[:, :, 1:2]).then_inc(srec_ready, 1)
                        if c:
                            dve.wait_ge(srec_ready, k + n0)
                            v.tensor_tensor(vext[:, s, :, 0:H], PS[:, 2 + 2 * s:4 + 2 * s, 2 * H:3 * H],
                                            vext[:, s, :, H:H + 1].broadcast_to([P, 2, H]), ALU.mult)\
                                .then_inc(v_copied, 2)
                    if live(k, 2, NB):
                        dve.wait_ge(kv_done, k + (n0 - 1))
                        wait_count(dve, ctx_done, k + (n0 - 3))
                        v.tensor_tensor(kvd[:, r, 0:H], KV[:, 0:H], headblock[:], ALU.mult).then_inc(kvd_ready, 1)
                        v.tensor_tensor(kvd[:, r, H:KVW], headcol[:], KV[:, H:H + 1].broadcast_to([P, NHEAD]),
                                        ALU.mult).then_inc(kvd_ready, 1)
                    add(3)
                    if live(k, 3, NB):
                        dve.wait_ge(attn_done, k + (n0 - 2))
                        for i in range(2):
                            stats((k - 3) * 2 + (i + c * CT), c)
                    if tile and live(k, COMB_B, CTB):
                        tile.stats()

                sweep(dve, 4, NB, 4, step, steps=4)
                dve.wait_ge(attn_done, n0 + NB)

            link(v.memset(parts_on[:], 0.0))
            for r in range(3):
                link(v.memset(parts_on[NE * r:NE * r + 1, :], 1.0))
            for s in range(2):
                link(v.memset(vext[:, s, :, H:H + 2], 1.0))
            for c in range(NCHUNK):
                for t in range(CT):
                    if c:
                        dve.wait_ge(x_rest_loaded, 16 * (NCHUNK - 1))
                    elif t % GT == 0:
                        dve.wait_ge(x_loaded[t // GT], 16)
                    stats(c * CT + t, c)
                slots, slots_to_rows, weights = route(c, c)
                slots(GT, CT)
                slots_to_rows(GT, CT)
                weights()
                if c == 0:
                    dve.wait_ge(b_loaded, 16 * NB12)
                    split(b1_f, b1_r, b1_p)
                    link(v.tensor_tensor(centre[:], centre[:], ident[:], ALU.add))
                    v.tensor_scalar(centre[:], centre[:], scale_col[:, 0:1], None, ALU.mult).then_inc(centre_ready, 1)
            dve.wait_ge(fold_done, 1)
            dve.wait_ge(attn_loaded, 16 * NATTN)
            v.tensor_copy(qkvW[:, 0:2 * H], PS[:, 6, 0:2 * H]).then_inc(fold_copied, 1)
            v.tensor_tensor(abias_f[:, 0:2 * H], abias_f[:, 0:2 * H], PS[0:96, 7, 0:2 * H], ALU.add).then_inc(fold_copied, 1)

            dve.wait_ge(fold_copied, 2)
            split(abias_f, abias_r, abias_p)

            def add_b2(f):
                first, stop = f * NCHUNK * NRG, (f + 1) * NCHUNK * NRG

                def weigh(n):
                    t = n % (NCHUNK * NRG) * GT * TOPK
                    if n >= NRG:
                        dve.wait_ge(b2_turned, n - NRG + 1)
                    v.tensor_tensor(place[:, n % NRG * GW:(n % NRG + 1) * GW].rearrange("p (t e) -> p t e", e=NE),
                                    chosen[:, t * NE:(t + GT * TOPK) * NE].rearrange("p (t e) -> p t e", e=NE),
                                    wtop[:, t:t + GT * TOPK].rearrange("p (t o) -> p t o", o=1)
                                    .broadcast_to([P, GT * TOPK, NE]), ALU.mult).then_inc(weighted, 1)

                dve.wait_ge(base_done, CT * NCHUNK * (f + 1))
                weigh(first)
                weigh(first + 1)
                for n in range(first, stop):
                    if n + 2 < stop:
                        weigh(n + 2)
                    dve.wait_ge(b2_done, n + 1)
                    g = n - first
                    xt = X[:, g * GW:(g + 1) * GW]
                    v.tensor_tensor(xt, xt, PS[:, 4 + n % 2, :], ALU.add).then_inc(b2_added, 1)

            add_b2(0)
            experts(0)

            attention(0, NCHUNK)
            slots_a, rows_a, weights_a = route(NCHUNK, NCHUNK + 1, lambda: combine(NCHUNK - 1, CTB, CTB + 2))
            combine(NCHUNK - 1, CTB + 2, CT)
            attention(1, NCHUNK + 2, lambda: (slots_a(GT, CT), rows_a(GT, CT), weights_a()))
            slots_b, rows_b, weights_b = route(NCHUNK + 1, NCHUNK + 3)
            experts(1, [lambda: slots_b(GT, 2 * GT), lambda: slots_b(2 * GT, 3 * GT), lambda: slots_b(3 * GT, CT),
                        lambda: rows_b(GT, CT), weights_b])
            add_b2(1)
            combine(NPHASE - 1, 0, CT)

        @block.tensor
        def _(pe):
            te = nc.tensor

            def turn(dst, src, n):
                for q in range(n):
                    last = te.transpose(dst[:, q * P:(q + 1) * P], src[:, q * H:(q + 1) * H], ident[:])
                return last

            def route(ph):
                c = ph % NCHUNK

                def turned(q):
                    if q < NRG // 2:
                        pe.wait_ge(u_done, CT // 2 * ph + (q + 1) * GT)
                    else:
                        pe.wait_ge(u2_done, CT // 2 * (ph - 1) + (q + 1) * GT)
                    wait_count(pe, tT_done, ph * NRG + q - 1)
                    t0 = (c * CT + q * GT) * H
                    turn(TP[q % 2], U[:, t0:t0 + GW], GT).then_inc(uT_done, 1)

                def scores(q):
                    pe.wait_ge(tT_done, ph * NRG + q + 1)
                    if ph == q == 0:
                        pe.wait_ge(bias_ready, 1)
                    wait_count(pe, topi_done, (ph * NRG + q - 1) * GT)
                    te.matmul(LOG[q % 2].rearrange("p (t e) -> p t e", e=NE), parts_on[:],
                              gb_p[:].rearrange("p (o e) -> p o e", o=1).broadcast_to([96, GT, NE]), start=True, stop=False)
                    for i in range(GT):
                        last = te.matmul(LOG[q % 2][:, i * NE:(i + 1) * NE], tT[:, q % 2, i * P:(i + 1) * P], gw[:],
                                         start=False, stop=(i == GT - 1))
                    last.then_inc(logits_done, 1)

                def rank(q):
                    pe.wait_ge(mask_ready, ph * NRG + q + 1)
                    if q == 0:
                        wait_count(pe, route_done, ph)
                    for i in range(q * GT, (q + 1) * GT):
                        m = mask[:, i * NE:(i + 1) * NE]
                        n = CT - 1 - i
                        te.matmul(RANK[:, i * NE:(i + 1) * NE], before[:], m, start=(i == 0), stop=(i in (0, CT - 1)))
                        if n:
                            te.matmul(RANK[:, (i + 1) * NE:CT * NE].rearrange("p (t e) -> p t e", e=NE), ones[:],
                                      m.rearrange("p (o e) -> p o e", o=1).broadcast_to([P, n, NE]),
                                      start=(i == 0), stop=False)
                        last = te.matmul(CNT, m, ones[:, 0:1], start=(i == 0), stop=(i == CT - 1))
                    return last

                turned(0)
                for q in range(NRG):
                    if q + 1 < NRG:
                        turned(q + 1)
                    scores(q)
                    if q >= 2:
                        rank(q - 2)
                rank(NRG - 2)
                rank(NRG - 1).then_inc(counted, 1)
                pe.wait_ge(ntiles_ready, ph + 1)
                te.matmul(SPAN, ends[:], ntiles[:], start=True, stop=True)
                te.matmul(BASE, ntiles[:, 0:1].broadcast_to([NE, P]), starts128[:], start=True, stop=True)\
                    .then_inc(spans_done, 1)
                pe.wait_ge(ended_ready, ph + 1)
                pe.wait_ge(based, 2 * ph + 2)
                te.matmul(EID, ones[0:NE, 0:1], ended[:], start=True, stop=True).then_inc(eid_done, 1)

            def experts(f):
                g0 = f * NGF

                def experts_of(g):
                    _, es = nc.values_load_multi_w_load_instructions(
                        eid[0:1, bass.ds(g * GT, GT)], engines=[te.engine], min_val=0, max_val=(NE - 1) * EW,
                        skip_runtime_bounds_check_because="the router cuts them to NE - 1 times EW")
                    return es

                def step(k, r, m):
                    s = 1 - r
                    if live(k, 0, NGF):
                        pe.wait_ge(xrow_loaded[r], (m + (g0 // 2 + 1)) * 16)
                        wait_count(pe, xT_ready, k + (g0 - 1))
                        turn(TP[r], xrow[:, r, :], GT).then_inc(x_turned, 1)
                    if live(k, 3, NGF):
                        pe.wait_ge(hid_ready, k + (g0 - 2))
                        wait_count(pe, hidT_ready, k + (g0 - 3))
                        turn(HT, hid[:, s, :], GT).then_inc(hid_turned, 1)
                    if live(k, 1, NGF):
                        es = experts_of(k - 1)
                        pe.wait_ge(xT_ready, k + g0)
                        wait_count(pe, glu_ready, k + (g0 - 2))
                        wait_count(pe, lin_ready, k + (g0 - 2))
                        for q in range(GT):
                            h1 = H1[s][:, q * 2 * H:(q + 1) * 2 * H]
                            last = te.matmul(h1, xT[:, s, q * P:(q + 1) * P], W[:, bass.ds(es[q], 2 * H)],
                                             start=True, stop=True)
                        last.then_inc(h1_done, 1)
                    if live(k, 3, NGF):
                        es = experts_of(k - 3)
                        pe.wait_ge(hidT_ready, k + (g0 - 2))
                        wait_count(pe, yrow_ready, k + (g0 - 3))
                        for q in range(GT):
                            y = YP[:, q * H:(q + 1) * H]
                            last = te.matmul(y, hidT[:, s, q * P:(q + 1) * P], W[:, bass.ds(es[q] + 2 * H, H)],
                                             start=True, stop=True)
                        last.then_inc(y_done, 1)

                sweep(pe, 8, NGF, 3, step, steps=8)

            def attention(c):
                n0 = c * NB

                def step(k, r, m):
                    s = 1 - r
                    if live(k, 1, NB):
                        pe.wait_ge(aT_ready, k + n0)
                        wait_count(pe, v_copied, (k + (n0 - 2)) * 2)
                        for i in range(2):
                            o = PS[:, 2 + 2 * s + i, 0:3 * H]
                            te.matmul(o, parts_on[:], abias_p[:], start=True, stop=False)
                            last = te.matmul(o, aT[:, s, i * P:(i + 1) * P], qkvW[:], start=False, stop=True)
                        last.then_inc(qkv_done, 1)
                    if live(k, 0, NB):
                        pe.wait_ge(arow_ready, (k + (n0 + 1)) * 2)
                        wait_count(pe, aT_ready, k + n0)
                        turn(PS[:, 0, :], arow[:, r, :], 2).then_inc(a_turned, 1)
                    if live(k, 2, NB):
                        pe.wait_ge(esm_ready, (k + (n0 - 1)) * 4)
                        wait_count(pe, qT_ready, k + (n0 - 2))
                        for i in range(2):
                            last = te.transpose(PS[:, 1, i * P:(i + 1) * P], esm[:, r, 2 * i, :], ident[:])
                        last.then_inc(q_turned, 1)
                    if live(k, 3, NB):
                        pe.wait_ge(kvd_ready, (k + (n0 - 2)) * 2)
                        pe.wait_ge(qT_ready, k + (n0 - 2))
                        wait_count(pe, attn_done, k + (n0 - 3))
                        for i in range(2):
                            last = te.matmul(CTX[:, i, :], qT[:, s, i * P:(i + 1) * P], kvd[:, s, :],
                                             start=True, stop=True)
                        last.then_inc(ctx_done, 1)
                    if live(k, 2, NB):
                        pe.wait_ge(v_copied, (k + (n0 - 1)) * 2)
                        wait_count(pe, kvd_ready, (k + (n0 - 2)) * 2)
                        for i in range(2):
                            last = te.matmul(KV, esm[:, r, 2 * i + 1, :], vext[:, r, i, :], start=(i == 0), stop=(i == 1))
                        last.then_inc(kv_done, 1)

                sweep(pe, 4, NB, 3, step, steps=4)

            pe.wait_ge(const_step, NCONST)
            pe.wait_ge(router_loaded, 16 * NROUTER)
            for c in range(NCHUNK):
                route(c)
            pe.wait_ge(attn_loaded, 16 * NATTN)
            for n, (w, wf) in enumerate(((wq_s, wfq_s), (wk_s, wfk_s))):
                te.matmul(PS[:, 6, n * H:(n + 1) * H], w[:], wf[:], start=True, stop=True)
            for n, wf in enumerate((wfq_s, wfk_s)):
                last = te.matmul(PS[0:96, 7, n * H:(n + 1) * H], bqk_s[:, n:n + 1].broadcast_to([P, 96]), wf[:],
                                 start=True, stop=True)
            last.then_inc(fold_done, 1)
            pe.wait_ge(route_done, NCHUNK)

            def add_b2(f):
                first, stop = f * NCHUNK * NRG, (f + 1) * NCHUNK * NRG

                def turned(n):
                    pe.wait_ge(weighted, n + 1)
                    wait_count(pe, b2_copied, n - 1)
                    turn(TP[n % 2], place[:, n % NRG * GW:(n % NRG + 1) * GW], GT).then_inc(b2_turned, 1)

                turned(first)
                for n in range(first, stop):
                    if n + 1 < stop:
                        turned(n + 1)
                    pe.wait_ge(b2_copied, n + 1)
                    wait_count(pe, b2_added, n - 1)
                    for i in range(GT):
                        last = te.matmul(PS[:, 4 + n % 2, i * H:(i + 1) * H], xT[:, n % 2, i * P:(i + 1) * P], b2_s[:],
                                         start=True, stop=True)
                    last.then_inc(b2_done, 1)

            pe.wait_ge(w_loaded, 16 * NW)
            pe.wait_ge(b1_spread, 16 * 3)
            pe.wait_ge(centre_ready, 1)

            def shift(k, r, m):
                wait_count(pe, w_ready, k - 1)
                o = PS[:, 2 + r, :].rearrange("p (e n) -> p e n", e=2)
                te.matmul(o, centre[:], w1_pair(k), start=True, stop=False)
                te.matmul(o, overH[:], b1_3[:, bass.ds(k * (4 * H), 4 * H)].rearrange("p (e n) -> p e n", e=2),
                          start=False, stop=True)\
                    .then_inc(shift_done, 1)

            sweep(pe, 2, NE // 2, 0, shift)
            pe.wait_ge(w_ready, NE // 2)
            pe.wait_ge(b_loaded, 16 * NB12)
            add_b2(0)
            pe.wait_ge(fold_copied, 2)

            for f in range(2):
                pe.wait_ge(route_done, (f + 1) * NCHUNK)
                if f == 0:
                    pe.wait_ge(b2_added, NCHUNK * NRG)
                experts(f)
                pe.wait_ge(yrow_ready, (f + 1) * NGF)
                if f == 1:
                    add_b2(1)
                if f == 0:
                    pe.wait_ge(bias_ready, 3)
                    for c in range(NCHUNK):
                        if c:
                            pe.wait_ge(route_done, NCHUNK + c)
                        attention(c)
                        route(NCHUNK + c)


def kernel(L0_attn_hidden_states, L0_attn_Wq, L0_attn_bq, L0_attn_Wk, L0_attn_bk, L0_attn_Wv, L0_attn_bv,
           L0_attn_Wfq, L0_attn_bfq, L0_attn_Wfk, L0_attn_bfk, L0_ffn_norm_scale, L0_ffn_gate_w, L0_ffn_gate_b,
           L0_ffn_w1, L0_ffn_b1, L0_ffn_w2, L0_ffn_b2):
    import numpy as np
    import concourse.bacc as bacc
    from concourse.bass_utils import run_bass_kernel_spmd

    arr = {n: np.asarray(a) for n, a in (
        ("x", L0_attn_hidden_states), ("wq", L0_attn_Wq), ("bq", L0_attn_bq), ("wk", L0_attn_Wk), ("bk", L0_attn_bk),
        ("wv", L0_attn_Wv), ("bv", L0_attn_bv), ("wfq", L0_attn_Wfq), ("bfq", L0_attn_bfq), ("wfk", L0_attn_Wfk),
        ("bfk", L0_attn_bfk), ("nscale", L0_ffn_norm_scale), ("gw", L0_ffn_gate_w), ("gb", L0_ffn_gate_b),
        ("w1", L0_ffn_w1), ("b1", L0_ffn_b1), ("w2", L0_ffn_w2), ("b2", L0_ffn_b2))}
    w1 = arr["w1"].reshape(NE, H, 2, H)
    laid = [
        ("x", arr["x"].reshape(NTOK, H)),
        ("wq", arr["wq"]), ("bq", arr["bq"].reshape(H, 1)), ("wk", arr["wk"]), ("bk", arr["bk"].reshape(H, 1)),
        ("wvT", arr["wv"].T), ("bv", arr["bv"]), ("wfqT", arr["wfq"].T), ("bfq", arr["bfq"]),
        ("wfkT", arr["wfk"].T), ("bfk", arr["bfk"]),
        ("nscale", arr["nscale"].reshape(H, 1)), ("gwT", arr["gw"].T), ("gate_b", arr["gb"]),
        ("w12T", np.concatenate([w1.transpose(3, 0, 2, 1).reshape(H, NE, 2 * H), arr["w2"].transpose(2, 0, 1)],
                                axis=2).reshape(H, NE * EW)),
        ("b1", arr["b1"].reshape(NE, H, 2).transpose(0, 2, 1).reshape(NE, 2 * H)), ("b2", arr["b2"]),
    ]
    nc = bacc.Bacc("TRN2", target_bir_lowering=False, num_devices=1)
    arrays, args = {}, []
    for name, a in laid:
        a = np.ascontiguousarray(a)
        arrays["in_" + name] = a
        args.append(nc.dram_tensor("in_" + name, a.shape, mybir.dt.from_np(a.dtype), kind="ExternalInput").ap())
    out = nc.dram_tensor("out", (NTOK, H), F32, kind="ExternalOutput").ap()
    xs = [nc.dram_tensor(f"xs{c}", (SLOTS, H), F32, kind="Internal").ap() for c in range(NCHUNK)]
    ys = [nc.dram_tensor(f"ys{c}", (SLOTS, H), F32, kind="Internal").ap() for c in range(NCHUNK)]
    build(nc, *args, out, xs, ys)
    r = run_bass_kernel_spmd(nc, [arrays], core_ids=[0])
    return r.results[0]["out"].reshape(16, 256, H)
```
